# Optimizing a Trainium2 kernel written in Bass

```python
import numpy as np
import jax
import jax.numpy as jnp

def _softmax(x, axis=-1):
    return jax.nn.softmax(x, axis=axis)

def _gelu(x):
    return jax.nn.gelu(x, approximate=True)

def _silu(x):
    return jax.nn.silu(x)

def _sigmoid(x):
    return jax.nn.sigmoid(x)

def _layernorm(x, axis=-1, eps=1e-05):
    m = jnp.mean(x, axis=axis, keepdims=True)
    v = jnp.var(x, axis=axis, keepdims=True)
    return (x - m) / jnp.sqrt(v + eps)

def _scatter_add(tgt, idx, src, axis=0):
    return tgt.at[idx].add(src)

def _segment_sum(src, seg, n):
    return jax.ops.segment_sum(src, seg, n)
kernel_name = 'mk_seq_preln_d1_jaxref_r8_f16ede'

def setup_inputs(seed: int=0):
    np.random.seed(seed)
    _w = jnp.asarray

    def _L0_attn_setup():
        import jax, jax.numpy as jnp
        import numpy as np
        D_MODEL = 256
        N_HEADS = 16
        HEAD_DIM = D_MODEL // N_HEADS
        SCALE = HEAD_DIM ** (-0.5)
        key = jax.random.key(seed)
        ks = jax.random.split(key, 9)
        B, L, D = (4, 512, D_MODEL)
        s = 1.0 / np.sqrt(D)
        inp = {'x': jax.random.normal(ks[0], (B, L, D), dtype=jnp.float32)}
        inp['Wq'] = jax.random.normal(ks[1], (D, D), dtype=jnp.float32) * s
        inp['bq'] = jnp.zeros((D,), dtype=jnp.float32)
        inp['Wk'] = jax.random.normal(ks[2], (D, D), dtype=jnp.float32) * s
        inp['bk'] = jnp.zeros((D,), dtype=jnp.float32)
        inp['Wv'] = jax.random.normal(ks[3], (D, D), dtype=jnp.float32) * s
        inp['bv'] = jnp.zeros((D,), dtype=jnp.float32)
        inp['Wo'] = jax.random.normal(ks[4], (D, D), dtype=jnp.float32) * s
        inp['bo'] = jnp.zeros((D,), dtype=jnp.float32)
        return inp
    _L0_attn_in = _L0_attn_setup()

    def _L0_ffn_setup():
        import jax, jax.numpy as jnp
        import numpy as np
        B, S, H = (4, 256, 256)
        INTER = 512
        E = 8
        TOPK = 2
        SHARED_I = INTER * 2

        def moe_forward(hidden_states, router_w, w1, w2, w_gate, w_up, w_down):
            b, s, h = hidden_states.shape
            x = hidden_states.reshape(-1, h)
            T = x.shape[0]
            logits = x @ router_w
            top_logits, top_indices = jax.lax.top_k(logits, TOPK)
            scores = jax.nn.softmax(top_logits, axis=-1)
            flat_idx = top_indices.reshape(-1)
            sorted_pos = jnp.argsort(flat_idx, stable=True)
            permuted = x[sorted_pos // TOPK]
            expert_ids = flat_idx[sorted_pos]
            out = jnp.zeros((T * TOPK, h), x.dtype)
            for e in range(E):
                mask = (expert_ids == e)[:, None]
                f1 = permuted * mask @ w1[e]
                g, u = jnp.split(f1, 2, axis=-1)
                act = jax.nn.silu(g) * u
                out = out + jnp.where(mask, act @ w2[e], 0.0)
            unperm = jnp.zeros_like(out).at[sorted_pos].set(out)
            combined = (unperm.reshape(T, TOPK, h) * scores[..., None]).sum(axis=1)
            shared = jax.nn.silu(x @ w_gate) * (x @ w_up) @ w_down
            return (combined + shared).reshape(b, s, h)
        key = jax.random.key(seed)
        ks = jax.random.split(key, 7)
        s = 0.02
        return {'hidden_states': jax.random.normal(ks[0], (B, S, H), jnp.float32), 'router_w': jax.random.normal(ks[1], (H, E), jnp.float32) * s, 'w1': jax.random.normal(ks[2], (E, H, 2 * INTER), jnp.float32) * s, 'w2': jax.random.normal(ks[3], (E, INTER, H), jnp.float32) * s, 'w_gate': jax.random.normal(ks[4], (H, SHARED_I), jnp.float32) * s, 'w_up': jax.random.normal(ks[5], (H, SHARED_I), jnp.float32) * s, 'w_down': jax.random.normal(ks[6], (SHARED_I, H), jnp.float32) * s}
    _L0_ffn_in = _L0_ffn_setup()
    _d = {'L0_attn_x': _L0_attn_in['x'], 'L0_attn_Wq': _L0_attn_in['Wq'], 'L0_attn_bq': _L0_attn_in['bq'], 'L0_attn_Wk': _L0_attn_in['Wk'], 'L0_attn_bk': _L0_attn_in['bk'], 'L0_attn_Wv': _L0_attn_in['Wv'], 'L0_attn_bv': _L0_attn_in['bv'], 'L0_attn_Wo': _L0_attn_in['Wo'], 'L0_attn_bo': _L0_attn_in['bo'], 'L0_ffn_router_w': _L0_ffn_in['router_w'], 'L0_ffn_w1': _L0_ffn_in['w1'], 'L0_ffn_w2': _L0_ffn_in['w2'], 'L0_ffn_w_gate': _L0_ffn_in['w_gate'], 'L0_ffn_w_up': _L0_ffn_in['w_up'], 'L0_ffn_w_down': _L0_ffn_in['w_down']}
    _x0 = _d['L0_attn_x']
    _d['L0_attn_x'] = jax.random.normal(jax.random.fold_in(jax.random.key(seed), 1), (8, 256, 256), dtype=_x0.dtype)
    del _x0
    return _d

def reference(L0_attn_x, L0_attn_Wq, L0_attn_bq, L0_attn_Wk, L0_attn_bk, L0_attn_Wv, L0_attn_bv, L0_attn_Wo, L0_attn_bo, L0_ffn_router_w, L0_ffn_w1, L0_ffn_w2, L0_ffn_w_gate, L0_ffn_w_up, L0_ffn_w_down):

    def _L0_attn_ref(x, Wq, bq, Wk, bk, Wv, bv, Wo, bo):
        import jax, jax.numpy as jnp
        import numpy as np
        D_MODEL = 256
        N_HEADS = 16
        HEAD_DIM = D_MODEL // N_HEADS
        SCALE = HEAD_DIM ** (-0.5)
        B, L, D = x.shape
        H, Hd = (N_HEADS, HEAD_DIM)
        q = jnp.einsum('bld,ed->ble', x, Wq) + bq
        k = jnp.einsum('bld,ed->ble', x, Wk) + bk
        v = jnp.einsum('bld,ed->ble', x, Wv) + bv
        phi_q = jax.nn.elu(q) + 1.0
        phi_k = jax.nn.elu(k) + 1.0
        phi_q = phi_q.reshape(B, L, H, Hd)
        phi_k = phi_k.reshape(B, L, H, Hd)
        v = v.reshape(B, L, H, Hd)
        kv_sum = jnp.cumsum(phi_k * v, axis=1)
        context = (phi_q * kv_sum).reshape(B, L, D) * SCALE
        return jnp.einsum('bld,ed->ble', context, Wo) + bo

    def _L0_ffn_ref(hidden_states, router_w, w1, w2, w_gate, w_up, w_down):
        import jax, jax.numpy as jnp
        import numpy as np
        B, S, H = (4, 256, 256)
        INTER = 512
        E = 8
        TOPK = 2
        SHARED_I = INTER * 2

        def moe_forward(hidden_states, router_w, w1, w2, w_gate, w_up, w_down):
            b, s, h = hidden_states.shape
            x = hidden_states.reshape(-1, h)
            T = x.shape[0]
            logits = x @ router_w
            top_logits, top_indices = jax.lax.top_k(logits, TOPK)
            scores = jax.nn.softmax(top_logits, axis=-1)
            flat_idx = top_indices.reshape(-1)
            sorted_pos = jnp.argsort(flat_idx, stable=True)
            permuted = x[sorted_pos // TOPK]
            expert_ids = flat_idx[sorted_pos]
            out = jnp.zeros((T * TOPK, h), x.dtype)
            for e in range(E):
                mask = (expert_ids == e)[:, None]
                f1 = permuted * mask @ w1[e]
                g, u = jnp.split(f1, 2, axis=-1)
                act = jax.nn.silu(g) * u
                out = out + jnp.where(mask, act @ w2[e], 0.0)
            unperm = jnp.zeros_like(out).at[sorted_pos].set(out)
            combined = (unperm.reshape(T, TOPK, h) * scores[..., None]).sum(axis=1)
            shared = jax.nn.silu(x @ w_gate) * (x @ w_up) @ w_down
            return (combined + shared).reshape(b, s, h)
        return moe_forward(hidden_states, router_w, w1, w2, w_gate, w_up, w_down)
    x = L0_attn_x
    x = x + _L0_attn_ref(_layernorm(x, axis=-1), L0_attn_Wq, L0_attn_bq, L0_attn_Wk, L0_attn_bk, L0_attn_Wv, L0_attn_bv, L0_attn_Wo, L0_attn_bo)
    x = x + _L0_ffn_ref(_layernorm(x, axis=-1), L0_ffn_router_w, L0_ffn_w1, L0_ffn_w2, L0_ffn_w_gate, L0_ffn_w_up, L0_ffn_w_down)
    return x

_drawn_inputs = setup_inputs


def setup_inputs(seed=0):
    import zlib

    import numpy as np

    out = dict(_drawn_inputs(seed))
    spreads = {'L0_attn_bq': (0.0, 0.1),
     'L0_attn_bk': (0.0, 0.1),
     'L0_attn_bv': (0.0, 0.1),
     'L0_attn_bo': (0.0, 0.721)}
    factors = {'L0_ffn_router_w': 8.0,
     'L0_ffn_w1': 8.0,
     'L0_ffn_w2': 8.0,
     'L0_ffn_w_gate': 8.0,
     'L0_ffn_w_up': 8.0,
     'L0_ffn_w_down': 8.0}
    for name, (base, spread) in spreads.items():
        noise = np.random.default_rng([zlib.crc32(name.encode()), seed]).standard_normal(out[name].shape)
        drawn = base * np.exp(spread * noise) if base else spread * noise
        out[name] = jnp.asarray(drawn.astype(out[name].dtype))
    for name, factor in factors.items():
        out[name] = (out[name] * factor).astype(out[name].dtype)
    return out
```

```python
from contextlib import ExitStack

import concourse.bass as bass
from concourse import mybir

ALU = mybir.AluOpType
ACT = mybir.ActivationFunctionType
AX = mybir.AxisListType
F32 = mybir.dt.float32
F16 = mybir.dt.float16
I32 = mybir.dt.int32
U32 = mybir.dt.uint32

P = 128
WS = 64.0
CS = 1.0 / 16.0
EPS = 1e-5


def layer_kernel(nc, x, w_att, w_bias, w_bo, w_shared, w_expert, out):
    B, L, D = x.shape
    NT = B * L // P
    TB = L // P
    KC = D // P
    HEAD_DIM = 16
    SCALE = float(HEAD_DIM) ** -0.5
    E = w_expert.shape[0]
    FS = w_shared.shape[2] // KC
    NP = FS // (2 * P)
    FE = w_expert.shape[2] // (2 * KC + D // P)
    FC = FE // P
    W1 = KC * 2 * FE
    NBLK = (2 * NT * P + E * (P - 1)) // P
    NBP = NBLK + 1
    BIG = 2 * NT * P
    AW = w_att.shape[1]

    scratch = nc.dram_tensor("xn2_rows", (NT * P, D), F32, kind="Internal").ap()
    xv = x.rearrange("b (t p) d -> b p t d", p=P)
    out_rows = out.rearrange("b l d -> (b l) d")
    outv = out.rearrange("b (t p) d -> b p t d", p=P)
    scr_v = scratch.rearrange("(b t p) d -> b p t d", p=P, t=TB)

    with ExitStack() as ctx:
        def sb(name, shape, dt=F32):
            return ctx.enter_context(nc.sbuf_tensor(name, shape, dt))

        def bank(name):
            return ctx.enter_context(nc.psum_tensor(name, [P, 512], F32))

        def sem(name):
            return ctx.enter_context(nc.semaphore(name))

        wa_h, wa_l = sb("wa_h", [P, AW], F16), sb("wa_l", [P, AW], F16)
        ws_h, ws_l = sb("ws_h", [P, 3, KC * FS], F16), sb("ws_l", [P, 3, KC * FS], F16)
        EW = w_expert.shape[2]
        we_h, we_l = sb("we_h", [P, E, EW], F16), sb("we_l", [P, E, EW], F16)
        stage = sb("stage", [P, EW])
        stage_att = we_l[:, E - 2:E, :].rearrange("p e n -> p (e n)").bitcast(F32)[:, 0:AW]
        stage_sh = we_h[:, E // 2:E, :].rearrange("p e n -> p (e n)").bitcast(F32)[:, 0:3 * KC * FS]

        def att_w(w, m):
            return w[:, m * KC * D:(m + 1) * KC * D].rearrange("p (k n) -> p k n", k=KC)

        def router_w(w):
            return w[:, 4 * KC * D:4 * KC * D + KC * E].rearrange("p (k n) -> p k n", k=KC)

        ident = sb("ident", [P, P])
        tri = sb("tri", [P, P], F16)
        ones16 = sb("ones16", [P, P], F16)
        keep = sb("keep", [P, 2, L], F16)
        minus_half = sb("minus_half", [P, TB])
        iota_i = sb("iota_i", [P, P], I32)
        iota_f = sb("iota_f", [P, P])
        iota16 = sb("iota16", [P, P], F16)
        tok_i = sb("tok_i", [P, NT], I32)
        tok_f = sb("tok_f", [P, NT])
        full_i = sb("full_i", [P, NT], I32)
        full_f = sb("full_f", [P, NT])

        xs = sb("xs", [P, NT, D])
        bias = sb("bias", [P, 3, KC])
        bias1 = sb("bias1", [P, 2, KC])
        bias_v = sb("bias_v", [P, KC])
        bo = sb("bo", [P, D])
        st = [sb(f"st{n}", [P, TB, 6]) for n in range(2)]
        mv = [sb(f"mv{n}", [P, TB, 2]) for n in range(2)]
        ve = [sb(f"ve{n}", [P, TB]) for n in range(2)]
        y0 = [sb(f"y0{n}", [P, TB]) for n in range(2)]
        nt_ = [sb(f"nt{n}", [P, TB]) for n in range(2)]
        nu = [sb(f"nu{n}", [P, TB]) for n in range(2)]
        rstd = [sb(f"rstd{n}", [P, TB]) for n in range(2)]
        xn = [sb(f"xn{n}", [P, TB, D]) for n in range(2)]
        xT_h = [sb(f"xTh{n}", [P, KC, L], F16) for n in range(2)]
        xT_l = [sb(f"xTl{n}", [P, KC, L], F16) for n in range(2)]
        work = sb("work", [P, 5, KC, L])
        ek, rk, eq, rq, kvs = (work[:, n, :, :] for n in range(5))
        phik, kv, phiq, cx = ek, rk, eq, rq
        cx_h, cx_l = sb("cx_h", [P, KC, L], F16), sb("cx_l", [P, KC, L], F16)
        sg = [sb(f"sg{n}", [P, 512]) for n in range(2)]
        ab = [sb(f"ab{n}", [P, 512]) for n in range(2)]
        ah = [sb(f"ah{n}", [P, 512], F16) for n in range(NP)]
        al = [sb(f"al{n}", [P, 512], F16) for n in range(NP)]

        logit = sb("logit", [P, TB, E])
        top = sb("top", [P, TB, 8])
        topi = sb("topi", [P, TB, 8], U32)
        best = sb("best", [P, 2, NT])
        ei = sb("ei", [P, 2, NT])
        sc_d, sc_e, sc_1 = sb("sc_d", [P, NT]), sb("sc_e", [P, NT]), sb("sc_1", [P, NT])
        score = sb("score", [P, 2, NT])
        oh = [sb(f"oh{k}", [P, NT, E]) for k in range(2)]
        member = sb("member", [P, E, NT], F16)
        by_expert = lambda a: a.rearrange("p (e t) -> p e t", e=E)
        before, total, run, cmp = (by_expert(xn[0][:, n // 2, (n % 2) * P:(n % 2 + 1) * P]) for n in range(4))
        s1, s2 = (by_expert(xT_h[0][:, n, :].bitcast(F32)) for n in range(2))
        s3 = by_expert(xT_l[0][:, 0, :].bitcast(F32))
        count, nblk, bend = sb("count", [P, E]), sb("nblk", [P, E]), sb("bend", [P, E])
        r1, r2, base = sb("r1", [P, E]), sb("r2", [P, E]), sb("base", [P, E])
        pick = [sb(f"pick{k}", [P, NT, E]) for k in range(2)]
        slot = sb("slot", [P, 2 * NT])
        slot_i, blk_i, pos_i = (sb(n, [P, 2 * NT], I32) for n in ("slot_i", "blk_i", "pos_i"))
        blk_f, pos_f = sb("blk_f", [P, 2 * NT]), sb("pos_f", [P, 2 * NT])
        sc16 = sb("sc16", [P, 2 * NT], F16)
        vals = sb("vals", [P, 3, 2 * NT])
        at_pos = stage[:].bitcast(F16)[:, 0:2 * NT * P].rearrange("p (n q) -> p n q", n=2 * NT)
        work16 = work[:].rearrange("p a k l -> p (a k l)").bitcast(F16)
        put = work16[:, 0:6 * NT * NBP].rearrange("p (n a b) -> p n a b", a=3, b=NBP)
        at_blk = work16[:, 6 * NT * NBP:8 * NT * NBP].rearrange("p (n b) -> p n b", b=NBP)
        bcmp = sb("bcmp", [P, NBP, E])
        bexp, bexp_c = sb("bexp", [P, NBP]), sb("bexp_c", [P, NBP])
        blk_expert = sb("blk_expert", [P, NBP], I32)
        src_f, pad_f, dst_f = sb("src_f", [P, NBP]), sb("pad_f", [P, NBP]), sb("dst_f", [P, NBP])
        src_row, dst_row = sb("src_row", [P, NBP], U32), sb("dst_row", [P, NBP], U32)
        slot_lo, slot_score = sb("slot_lo", [P, NBP]), sb("slot_score", [P, NBP])

        gi = [sb(f"gi{n}", [P, 1], U32) for n in range(2)]
        si = [sb(f"si{n}", [P, 1], U32) for n in range(2)]
        xg = [sb(f"xg{n}", [P, D]) for n in range(2)]
        gT_h = [cx_h[:, n, :].rearrange("p (k l) -> p k l", k=KC) for n in range(2)]
        gT_l = [cx_l[:, n, :].rearrange("p (k l) -> p k l", k=KC) for n in range(2)]
        ya = [xn[1][:, n, :] for n in range(2)]

        bT, bK, bV, bQ, bG, bU, bD, bR = (bank(n) for n in ("bT", "bK", "bV", "bQ", "bG", "bU", "bD", "bR"))

        names = """x0_in x_in att_in bias_in sh_in ex_in att_hi att_lo sh_hi sh_lo ex_hi ex_lo
            const_pool const_dve bias_done xn2_saved out_saved
            ln1_step ln2_step ve1 ve2 pow1 pow2 xn1 xn2 xbo
            t1 t1_hi t1_lo t2 t2_hi t2_lo k_ps v_ps q_ps ek_done rk_done eq_done rq_done
            phik_done kv_done kvs_done phiq_done cx_done cxh_done cxl_done wo_ps x1_done
            g_ps u_ps sg_done a_done ah_done al_done d_ps x2_done
            r_ps logit_done top_done topi_done best_done
            rt dscore escore member_done rank_ps put_done put_ps plan_done bexp_done
            gi_done gathered0 gathered1 tx_ps gh_done gl_done ta_ps o_ps y_done si_done scattered""".split()
        S = {n: sem(n) for n in names}

        block = ctx.enter_context(nc.Block())

        def product(pe, dst, lhs_h, lhs_l, rhs_h, rhs_l, n, first=True, last=True, lone=False):
            steps = [(lhs_h, rhs_h), (lhs_h, rhs_l), (lhs_l, rhs_h)]
            for s, (a, b) in enumerate(steps):
                for c in range(n):
                    ins = pe.matmul(dst, a(c), b(c), start=first and s == 0 and c == 0,
                                    stop=last and s == 2 and c == n - 1, skip_group_check=lone)
            return ins

        @block.sync
        def _(sp):
            sp.dma_start(xs[:, 0:TB, :], xv[0]).then_inc(S["x0_in"], 16)
            sp.dma_start(stage_att, w_att).then_inc(S["att_in"], 16)
            sp.dma_start(bias[:], w_bias).then_inc(S["bias_in"], 16)
            sp.dma_start(bo[:], w_bo.to_broadcast((P, D))).then_inc(S["bias_in"], 16)
            for b in range(1, B):
                sp.dma_start(xs[:, b * TB:(b + 1) * TB, :], xv[b]).then_inc(S["x_in"], 16)
            sp.dma_start(stage_sh, w_shared.rearrange("p m n -> p (m n)")).then_inc(S["sh_in"], 16)
            sp.dma_start(stage[:], w_expert[0]).then_inc(S["ex_in"], 16)

            def step(i, last):
                sp.wait_ge(S["xn2"], TB * (i + 1))
                sp.dma_start(scr_v[i] if isinstance(i, int) else scr_v[bass.ds(i, 1)].rearrange("o p t d -> (o p) t d"),
                             xn[1][:]).then_inc(S["xn2_saved"], 16)
                if not last:
                    sp.wait_ge(S["ex_hi"], 3 * (i + 1))
                    sp.wait_ge(S["ex_lo"], 3 * (i + 1))
                    src = w_expert[i + 1] if isinstance(i, int) else \
                        w_expert[bass.ds(i + 1, 1)].rearrange("o p n -> (o p) n")
                    sp.dma_start(stage[:], src).then_inc(S["ex_in"], 16)

            def save(i):
                sp.wait_ge(S["x2_done"], i + 1)
                dst = outv[i] if isinstance(i, int) else outv[bass.ds(i, 1)].rearrange("o p t d -> (o p) t d")
                sp.dma_start(dst, xs[:, bass.ds(TB * i, TB), :]).then_inc(S["out_saved"], 16)

            step(0, False)
            step(1, False)
            with sp.Fori(2, B - 1) as i:
                save(i - 2)
                step(i, False)
            save(B - 3)
            step(B - 1, True)
            save(B - 2)
            save(B - 1)
            sp.wait_ge(S["out_saved"], 16 * B)
            sp.wait_ge(S["scattered"], 16 * NBLK)

        @block.gpsimd
        def _(pool):
            pool.memset(ident[:], 0.0).then_inc(S["const_pool"], 1)
            pool.memset(ones16[:], 1.0).then_inc(S["const_pool"], 1)
            pool.memset(minus_half[:], -0.5).then_inc(S["const_pool"], 1)
            pool.iota(iota_i[:], pattern=[[1, P]], base=0, channel_multiplier=0).then_inc(S["const_pool"], 1)
            pool.iota(tok_i[:], pattern=[[P, NT]], base=1, channel_multiplier=1).then_inc(S["const_pool"], 1)
            pool.iota(full_i[:], pattern=[[P, NT]], base=0, channel_multiplier=0).then_inc(S["const_pool"], 1)
            pool.wait_ge(S["const_pool"], 6)
            pool.affine_select(out=ident[:], in_=ident[:], compare_op=ALU.not_equal, fill=1.0, base=0,
                               pattern=[[-1, P]], channel_multiplier=1).then_inc(S["const_pool"], 1)
            pool.affine_select(out=tri[:], in_=ones16[:], compare_op=ALU.is_ge, fill=0.0, base=-1,
                               pattern=[[1, P]], channel_multiplier=-1).then_inc(S["const_pool"], 1)

            def rsqrt(n, i):
                pool.wait_ge(S[f"ve{n + 1}"], i + 1)
                pool.tensor_tensor(y0[n][:], ve[n][:], minus_half[:], ALU.pow).then_inc(S[f"pow{n + 1}"], 1)

            def add_bo(i):
                pool.wait_ge(S["xn1"], TB * (i + 1))
                xi = xs[:, bass.ds(TB * i, TB), :]
                pool.tensor_tensor(xi, xi, bo[:].rearrange("p (o d) -> p o d", o=1).to_broadcast((P, TB, D)),
                                   ALU.add).then_inc(S["xbo"], 1)

            rsqrt(0, 0)
            pool.wait_ge(S["bias_in"], 32)
            add_bo(0)
            with pool.Fori(0, B - 1) as i:
                rsqrt(0, i + 1)
                add_bo(i + 1)
                rsqrt(1, i)
            rsqrt(1, B - 1)

            pool.wait_ge(S["plan_done"], 3)
            pool.wait_ge(S["xn2_saved"], 16 * B)

            def gather(b, q, fresh):
                if not fresh:
                    pool.wait_ge(S["tx_ps"], b - 1)
                pool.tensor_copy(gi[q][:], src_row[:, bass.ds(b, 1)]).then_inc(S["gi_done"], 1)
                pool.wait_ge(S["gi_done"], b + 1)
                pool.nop(nofuse=True)
                pool.indirect_dma_start(xg[q][:], None, scratch, bass.IndirectOffsetOnAxis(ap=gi[q][:], axis=0)
                                        ).then_inc(S[f"gathered{q}"], 16)

            def scatter(b, q):
                pool.wait_ge(S["scattered"], 16 * b)
                pool.tensor_copy(si[q][:], dst_row[:, bass.ds(b, 1)]).then_inc(S["si_done"], 1)
                pool.wait_ge(S["si_done"], b + 1)
                pool.wait_ge(S["y_done"], b + 1)
                pool.nop(nofuse=True)
                pool.indirect_dma_start(out_rows, bass.IndirectOffsetOnAxis(ap=si[q][:], axis=0), ya[q], None,
                                        bounds_check=NT * P - 1, oob_is_err=False, compute_op=ALU.add
                                        ).then_inc(S["scattered"], 16)

            gather(0, 0, True)
            gather(1, 1, True)
            pool.wait_ge(S["out_saved"], 16 * B)
            with pool.Fori(0, NBLK - 3, 2) as b:
                for q in range(2):
                    gather(b + 2 + q, q, False)
                    scatter(b + q, q)
            gather(NBLK - 1, 0, False)
            scatter(NBLK - 3, 0)
            scatter(NBLK - 2, 1)
            scatter(NBLK - 1, 0)

        @block.tensor
        def _(pe):
            def norm_T(n, i):
                pe.wait_ge(S[f"xn{n + 1}"], TB * (i + 1))
                if n == 0:
                    if not isinstance(i, int) or i >= 2:
                        pe.wait_ge(S["t2_lo"], i - 1)
                    if not isinstance(i, int) or i >= 1:
                        pe.wait_ge(S["t1_lo"], i)
                else:
                    pe.wait_ge(S["t1_lo"], i + 1 if isinstance(i, int) and i == B - 1 else i + 2)
                for t in range(TB):
                    for k in range(KC):
                        ins = pe.transpose(bT[:, k * L + t * P:k * L + (t + 1) * P],
                                           xn[n][:, t, k * P:(k + 1) * P], ident[:])
                ins.then_inc(S[f"t{n + 1}"], 1)

            def project(i):
                pe.wait_ge(S["t1_hi"], i + 1)
                pe.wait_ge(S["t1_lo"], i + 1)
                for m, dst, done in ((1, bK, "k_ps"), (2, bV, "v_ps"), (0, bQ, "q_ps")):
                    if not isinstance(i, int) or i >= 1:
                        if m == 1:
                            pe.wait_ge(S["x1_done"], i)
                        elif m == 2:
                            pe.wait_ge(S["kv_done"], KC * i)
                        else:
                            pe.wait_ge(S["eq_done"], KC * i)
                            pe.wait_ge(S["rq_done"], KC * i)
                    wh, wl = att_w(wa_h, m), att_w(wa_l, m)
                    for c in range(KC):
                        ins = product(pe, dst[:, c * L:(c + 1) * L],
                                      lambda k: wh[:, k, c * P:(c + 1) * P], lambda k: wl[:, k, c * P:(c + 1) * P],
                                      lambda k: xT_h[0][:, k, :], lambda k: xT_l[0][:, k, :], KC)
                    ins.then_inc(S[done], 1)

            def attend_out(i):
                pe.wait_ge(S["cxh_done"], i + 1)
                pe.wait_ge(S["cxl_done"], i + 1)
                pe.wait_ge(S["ek_done"], KC * (i + 1))
                pe.wait_ge(S["rk_done"], KC * (i + 1))
                wh, wl = att_w(wa_h, 3), att_w(wa_l, 3)
                for t in range(TB):
                    ins = product(pe, bK[:, t * D:(t + 1) * D],
                                  lambda k: cx_h[:, k, t * P:(t + 1) * P], lambda k: cx_l[:, k, t * P:(t + 1) * P],
                                  lambda k: wh[:, k, :], lambda k: wl[:, k, :], KC)
                ins.then_inc(S["wo_ps"], 1)

            def route(i):
                pe.wait_ge(S["t2_hi"], i + 1)
                pe.wait_ge(S["t2_lo"], i + 1)
                if not isinstance(i, int) or i >= 1:
                    pe.wait_ge(S["logit_done"], i)
                wh, wl = router_w(wa_h), router_w(wa_l)
                for t in range(TB):
                    ins = product(pe, bR[:, t * E:(t + 1) * E],
                                  lambda k: xT_h[1][:, k, t * P:(t + 1) * P], lambda k: xT_l[1][:, k, t * P:(t + 1) * P],
                                  lambda k: wh[:, k, :], lambda k: wl[:, k, :], KC)
                ins.then_inc(S["r_ps"], 1)

            def gate_up(i, f):
                n = NP * i + f
                for m, dst, done, free in ((0, bG, "g_ps", "sg_done"), (1, bU, "u_ps", "a_done")):
                    if not isinstance(i, int) or n >= 1:
                        pe.wait_ge(S[free], n)
                    wh = ws_h[:, m, :].rearrange("p (k n) -> p k n", k=KC)
                    wl = ws_l[:, m, :].rearrange("p (k n) -> p k n", k=KC)
                    for c in range(2):
                        at = (2 * f + c) * P
                        ins = product(pe, dst[:, c * L:(c + 1) * L],
                                      lambda k: wh[:, k, at:at + P], lambda k: wl[:, k, at:at + P],
                                      lambda k: xT_h[1][:, k, :], lambda k: xT_l[1][:, k, :], KC)
                    ins.then_inc(S[done], 1)

            def down(i, f):
                pe.wait_ge(S["ah_done"], NP * i + f + 1)
                pe.wait_ge(S["al_done"], NP * i + f + 1)
                if f == 0 and (not isinstance(i, int) or i >= 1):
                    pe.wait_ge(S["x2_done"], i)
                wh = ws_h[:, 2, :].rearrange("p (c n) -> p c n", n=D)
                wl = ws_l[:, 2, :].rearrange("p (c n) -> p c n", n=D)
                for t in range(TB):
                    ins = product(pe, bD[:, t * D:(t + 1) * D],
                                  lambda c: ah[f][:, c * L + t * P:c * L + (t + 1) * P],
                                  lambda c: al[f][:, c * L + t * P:c * L + (t + 1) * P],
                                  lambda c: wh[:, 2 * f + c, :], lambda c: wl[:, 2 * f + c, :], 2,
                                  first=(f == 0 and t == 0), last=(f == NP - 1), lone=True)
                ins.then_inc(S["d_ps"], 1)

            def step(i, shared, ahead):
                if shared:
                    route(i - 1)
                project(i)
                if ahead:
                    norm_T(0, i + 1)
                if shared:
                    gate_up(i - 1, 0)
                    gate_up(i - 1, 1)
                    down(i - 1, 0)
                    gate_up(i - 1, 2)
                    down(i - 1, 1)
                attend_out(i)
                if shared:
                    gate_up(i - 1, 3)
                    down(i - 1, 2)
                norm_T(1, i)
                if shared:
                    down(i - 1, 3)

            pe.wait_ge(S["const_pool"], 8)
            norm_T(0, 0)
            pe.wait_ge(S["att_hi"], 1)
            pe.wait_ge(S["att_lo"], 1)
            step(0, False, True)
            pe.wait_ge(S["sh_hi"], 3)
            pe.wait_ge(S["sh_lo"], 3)
            step(1, True, True)
            with pe.Fori(2, B - 1) as i:
                step(i, True, True)
            step(B - 1, True, False)
            route(B - 1)
            gate_up(B - 1, 0)
            gate_up(B - 1, 1)
            down(B - 1, 0)
            pe.wait_ge(S["member_done"], 1)
            pe.wait_ge(S["eq_done"], KC * B)
            pe.wait_ge(S["rq_done"], KC * B)
            mem = member[:].rearrange("p e t -> p (e t)")
            pe.matmul(bQ[:, 0:P], tri[:], mem, start=True, stop=True)
            pe.matmul(bQ[:, P:2 * P], ones16[:], mem, start=True, stop=True).then_inc(S["rank_ps"], 1)
            gate_up(B - 1, 2)
            down(B - 1, 1)
            gate_up(B - 1, 3)
            down(B - 1, 2)
            down(B - 1, 3)
            pe.wait_ge(S["put_done"], 1)
            for n in range(2 * NT):
                ins = pe.matmul(bV[:, 0:3 * NBP], at_pos[:, n, :], put[:, n, :, :].rearrange("p a b -> p (a b)"),
                                start=(n == 0), stop=(n == 2 * NT - 1))
            ins.then_inc(S["put_ps"], 1)

            def turn_x(b, q):
                pe.wait_ge(S[f"gathered{q}"], 8 * (b - q) + 16)
                if not isinstance(b, int) or b >= 1:
                    pe.wait_ge(S["gl_done"], b)
                for k in range(KC):
                    ins = pe.transpose(bT[:, k * P:(k + 1) * P], xg[q][:, k * P:(k + 1) * P], ident[:])
                ins.then_inc(S["tx_ps"], 1)

            def turn_a(b, q):
                pe.wait_ge(S["a_done"], NP * B + b + 1)
                if not isinstance(b, int) or b >= 1:
                    pe.wait_ge(S["al_done"], NP * B + b)
                for c in range(FC):
                    ins = pe.transpose(bK[:, c * P:(c + 1) * P], ab[q][:, c * P:(c + 1) * P], ident[:])
                ins.then_inc(S["ta_ps"], 1)

            def expert_up(b, q, e, half):
                dst, done, free = ((bG, "g_ps", "sg_done"), (bU, "u_ps", "a_done"))[half]
                pe.wait_ge(S[free], NP * B + b)
                if half == 0:
                    pe.wait_ge(S["gh_done"], b + 1)
                    pe.wait_ge(S["gl_done"], b + 1)
                w = [a[:, bass.ds(e, 1), 0:W1].rearrange("p o (k h n) -> p (o k) h n", k=KC, h=2) for a in (we_h, we_l)]
                product(pe, dst[:], lambda k: gT_h[q][:, k, :], lambda k: gT_l[q][:, k, :],
                        lambda k: w[0][:, k, half, :], lambda k: w[1][:, k, half, :], KC).then_inc(S[done], 1)

            def expert_down(b, q, e):
                pe.wait_ge(S["ah_done"], NP * B + b + 1)
                pe.wait_ge(S["al_done"], NP * B + b + 1)
                if not isinstance(b, int) or b >= 2:
                    pe.wait_ge(S["y_done"], b - 1)
                w = [a[:, bass.ds(e, 1), W1:EW].rearrange("p o (c n) -> p (o c) n", n=D) for a in (we_h, we_l)]
                dst = (bV, bQ)[q][:, 0:D]
                product(pe, dst, lambda c: ah[q][:, c * P:(c + 1) * P], lambda c: al[q][:, c * P:(c + 1) * P],
                        lambda c: w[0][:, c, :], lambda c: w[1][:, c, :], FC).then_inc(S["o_ps"], 1)

            def expert_of(b):
                return pe.value_load(blk_expert[0:1, bass.ds(b, 1)], min_val=0, max_val=E - 1)

            def routed(b, q, first, last):
                e = expert_of(b)
                expert_up(b, q, e, 0)
                if not first:
                    turn_a(b - 1, 1 - q)
                if not last:
                    turn_x(b + 1, 1 - q)
                expert_up(b, q, e, 1)
                if not first:
                    expert_down(b - 1, 1 - q, expert_of(b - 1))

            pe.wait_ge(S["bexp_done"], 1)
            pe.wait_ge(S["ex_hi"], 3 * E)
            pe.wait_ge(S["ex_lo"], 3 * E)
            pe.wait_ge(S["plan_done"], 3)
            pe.wait_ge(S["t2_lo"], B)
            pe.wait_ge(S["x1_done"], B)
            turn_x(0, 0)
            routed(0, 0, True, False)
            routed(1, 1, False, False)
            routed(2, 0, False, False)
            with pe.Fori(3, NBLK - 2, 2) as b:
                routed(b, 1, False, False)
                routed(b + 1, 0, False, False)
            routed(NBLK - 2, 1, False, False)
            routed(NBLK - 1, 0, False, True)
            turn_a(NBLK - 1, 0)
            expert_down(NBLK - 1, 0, expert_of(NBLK - 1))

        @block.scalar
        def _(act):
            def split_hi(n, i):
                act.wait_ge(S[f"t{n + 1}"], i + 1)
                if not isinstance(i, int) or i >= 1:
                    if n == 0:
                        act.wait_ge(S["q_ps"], i)
                    else:
                        act.wait_ge(S["r_ps"], i)
                        act.wait_ge(S["u_ps"], NP * i)
                act.activation(xT_h[n][:].rearrange("p k l -> p (k l)"), bT[:], ACT.Copy).then_inc(S[f"t{n + 1}_hi"], 1)

            def exps(i):
                for src, ready, e, r, m, ed, rd, used in ((bK, "k_ps", ek, rk, 1, "ek_done", "rk_done", "kvs_done"),
                                                          (bQ, "q_ps", eq, rq, 0, "eq_done", "rq_done", "cxl_done")):
                    act.wait_ge(S[ready], i + 1)
                    if not isinstance(i, int) or i >= 1:
                        act.wait_ge(S[used], i)
                    for c in range(KC):
                        act.activation(e[:, c, :], src[:, c * L:(c + 1) * L], ACT.Exp, bias=bias[:, m, c:c + 1],
                                       scale=1.0 / WS).then_inc(S[ed], 1)
                    for c in range(KC):
                        act.activation(r[:, c, :], src[:, c * L:(c + 1) * L], ACT.Identity, bias=bias1[:, m, c:c + 1],
                                       scale=1.0 / WS).then_inc(S[rd], 1)

            def context_hi(i):
                act.wait_ge(S["cx_done"], i + 1)
                if not isinstance(i, int) or i >= 1:
                    act.wait_ge(S["wo_ps"], i)
                act.activation(cx_h[:], cx, ACT.Copy).then_inc(S["cxh_done"], 1)

            def silu(n, q):
                act.wait_ge(S["g_ps"], n + 1)
                act.wait_ge(S["a_done"], n)
                act.activation(sg[q][:], bG[:], ACT.Silu, scale=1.0 / WS).then_inc(S["sg_done"], 1)

            def act_hi(i, f):
                n = NP * i + f
                act.wait_ge(S["a_done"], n + 1)
                if not isinstance(i, int) or i >= 1:
                    act.wait_ge(S["d_ps"], n - NP + 1)
                act.activation(ah[f][:], ab[f % 2][:], ACT.Copy).then_inc(S["ah_done"], 1)

            def expert_hi(e, j):
                if j == 0:
                    act.wait_ge(S["ex_in"], 16 * (e + 1))
                    if isinstance(e, int) and e == E // 2:
                        act.wait_ge(S["sh_lo"], 3)
                part = slice(j * EW // 3, (j + 1) * EW // 3)
                act.activation(we_h[:, bass.ds(e, 1), part].rearrange("p o n -> p (o n)"), stage[:, part], ACT.Copy,
                               scale=WS).then_inc(S["ex_hi"], 1)

            def shared(i, f):
                silu(NP * i + f, f % 2)
                act_hi(i, f)

            def step(i, sh, ahead):
                exps(i)
                if ahead:
                    split_hi(0, i + 1)
                context_hi(i)
                if sh:
                    shared(i - 1, 0)
                expert_hi(i, 0)
                if sh:
                    shared(i - 1, 1)
                expert_hi(i, 1)
                if sh:
                    shared(i - 1, 2)
                expert_hi(i, 2)
                if sh:
                    shared(i - 1, 3)
                split_hi(1, i)

            act.wait_ge(S["att_in"], 16)
            act.activation(wa_h[:], stage_att, ACT.Copy, scale=WS).then_inc(S["att_hi"], 1)
            split_hi(0, 0)
            act.wait_ge(S["bias_done"], 2)
            act.wait_ge(S["sh_in"], 16)
            M = KC * FS
            for m in range(3):
                act.activation(ws_h[:, m, :], stage_sh[:, m * M:(m + 1) * M], ACT.Copy, scale=WS).then_inc(S["sh_hi"], 1)
            act.wait_ge(S["sh_lo"], 3)
            act.wait_ge(S["att_lo"], 1)
            step(0, False, True)
            step(1, True, True)
            with act.Fori(2, B - 1) as i:
                step(i, True, True)
            step(B - 1, True, False)
            shared(B - 1, 0)
            act.wait_ge(S["dscore"], 1)
            act.activation(sc_e[:], sc_d[:], ACT.Exp).then_inc(S["escore"], 1)
            for f in range(1, NP):
                shared(B - 1, f)

            def gather_hi(b, q):
                act.wait_ge(S["tx_ps"], b + 1)
                if not isinstance(b, int) or b >= 2:
                    act.wait_ge(S["u_ps"], NP * B + b - 1)
                act.activation(gT_h[q].rearrange("p k l -> p (k l)"), bT[:, 0:KC * P], ACT.Copy).then_inc(S["gh_done"], 1)

            def routed_act_hi(b, q):
                act.wait_ge(S["ta_ps"], b + 1)
                if isinstance(b, int) and b < 2:
                    act.wait_ge(S["d_ps"], NP * B)
                else:
                    act.wait_ge(S["o_ps"], b - 1)
                act.activation(ah[q][:], bK[:], ACT.Copy).then_inc(S["ah_done"], 1)

            def routed(b, q, first, last):
                silu(NP * B + b, q)
                if not first:
                    routed_act_hi(b - 1, 1 - q)
                if not last:
                    gather_hi(b + 1, 1 - q)

            gather_hi(0, 0)
            routed(0, 0, True, False)
            routed(1, 1, False, False)
            routed(2, 0, False, False)
            with act.Fori(3, NBLK - 2, 2) as b:
                routed(b, 1, False, False)
                routed(b + 1, 0, False, False)
            routed(NBLK - 2, 1, False, False)
            routed(NBLK - 1, 0, False, True)
            routed_act_hi(NBLK - 1, 0)

        @block.vector
        def _(dve):
            LN = 7

            def norm(n, i):
                s = S[f"ln{n + 1}_step"]
                at = LN * i
                for t in range(TB):
                    dve.bn_stats(st[n][:, t, :], xs[:, bass.ds(TB * i + t, 1), :].rearrange("p o d -> p (o d)")).then_inc(s, 1)
                dve.wait_ge(s, at + 2)
                dve.nop(nofuse=True)
                for t in range(TB):
                    dve.bn_aggr(mv[n][:, t, :], st[n][:, t, :]).then_inc(s, 1)
                dve.wait_ge(s, at + 4)
                dve.tensor_scalar(ve[n][:], mv[n][:, :, 1], EPS, None, ALU.add).then_inc(S[f"ve{n + 1}"], 1)

            def norm_apply(n, i):
                s = S[f"ln{n + 1}_step"]
                at = LN * i
                dve.wait_ge(S[f"pow{n + 1}"], i + 1)
                dve.tensor_tensor(nt_[n][:], y0[n][:], y0[n][:], ALU.mult).then_inc(s, 1)
                dve.wait_ge(s, at + 5)
                dve.scalar_tensor_tensor(out=nu[n][:], in0=nt_[n][:], scalar=-0.5, in1=ve[n][:], op0=ALU.mult,
                                         op1=ALU.mult).then_inc(s, 1)
                dve.wait_ge(s, at + 6)
                dve.scalar_tensor_tensor(out=rstd[n][:], in0=nu[n][:], scalar=1.5, in1=y0[n][:], op0=ALU.add,
                                         op1=ALU.mult).then_inc(s, 1)
                dve.wait_ge(s, at + 7)
                if not isinstance(i, int) or i >= 1:
                    dve.wait_ge(S[f"t{n + 1}"], i)
                    if n == 1:
                        dve.wait_ge(S["xn2_saved"], 16 * i)
                for t in range(TB):
                    dve.tensor_scalar(xn[n][:, t, :], xs[:, bass.ds(TB * i + t, 1), :].rearrange("p o d -> p (o d)"),
                                      mv[n][:, t, 0:1], rstd[n][:, t:t + 1], ALU.subtract, ALU.mult
                                      ).then_inc(S[f"xn{n + 1}"], 1)

            def split_lo(n, i):
                dve.wait_ge(S[f"t{n + 1}_hi"], i + 1)
                dve.tensor_tensor(xT_l[n][:].rearrange("p k l -> p (k l)"), bT[:],
                                  xT_h[n][:].rearrange("p k l -> p (k l)"), ALU.subtract).then_inc(S[f"t{n + 1}_lo"], 1)

            def keys(i):
                dve.wait_ge(S["ek_done"], KC * (i + 1))
                dve.wait_ge(S["rk_done"], KC * (i + 1))
                dve.scalar_tensor_tensor(out=phik, in0=ek, scalar=1.0, in1=rk, op0=ALU.min, op1=ALU.max
                                         ).then_inc(S["phik_done"], 1)
                dve.wait_ge(S["phik_done"], i + 1)
                dve.wait_ge(S["v_ps"], i + 1)
                for c in range(KC):
                    dve.scalar_tensor_tensor(out=kv[:, c, :], in0=bV[:, c * L:(c + 1) * L], scalar=bias_v[:, c:c + 1],
                                             in1=phik[:, c, :], op0=ALU.add, op1=ALU.mult).then_inc(S["kv_done"], 1)
                dve.wait_ge(S["kv_done"], KC * (i + 1))
                dve.tensor_tensor_scan(kvs.rearrange("p k l -> p (k l)"), keep[:].rearrange("p k l -> p (k l)"),
                                       kv.rearrange("p k l -> p (k l)"), 0.0, ALU.mult, ALU.add
                                       ).then_inc(S["kvs_done"], 1)

            def queries(i):
                dve.wait_ge(S["eq_done"], KC * (i + 1))
                dve.wait_ge(S["rq_done"], KC * (i + 1))
                dve.scalar_tensor_tensor(out=phiq, in0=eq, scalar=1.0, in1=rq, op0=ALU.min, op1=ALU.max
                                         ).then_inc(S["phiq_done"], 1)
                dve.wait_ge(S["phiq_done"], i + 1)
                dve.wait_ge(S["kvs_done"], i + 1)
                if not isinstance(i, int) or i >= 1:
                    dve.wait_ge(S["cxh_done"], i)
                dve.scalar_tensor_tensor(out=cx, in0=kvs, scalar=SCALE * CS / WS, in1=phiq, op0=ALU.mult,
                                         op1=ALU.mult).then_inc(S["cx_done"], 1)

            def context_lo(i):
                dve.wait_ge(S["cxh_done"], i + 1)
                dve.tensor_tensor(cx_l[:], cx, cx_h[:], ALU.subtract).then_inc(S["cxl_done"], 1)

            def residual(i):
                dve.wait_ge(S["wo_ps"], i + 1)
                dve.wait_ge(S["xbo"], i + 1)
                xi = xs[:, bass.ds(TB * i, TB), :]
                dve.scalar_tensor_tensor(out=xi, in0=bK[:].rearrange("p (t d) -> p t d", t=TB), scalar=1.0 / (WS * CS),
                                         in1=xi, op0=ALU.mult, op1=ALU.add).then_inc(S["x1_done"], 1)
                dve.wait_ge(S["x1_done"], i + 1)
                dve.nop(nofuse=True)

            def swiglu(n, q):
                dve.wait_ge(S["sg_done"], n + 1)
                dve.wait_ge(S["u_ps"], n + 1)
                dve.scalar_tensor_tensor(out=ab[q][:], in0=bU[:], scalar=1.0 / WS, in1=sg[q][:], op0=ALU.mult,
                                         op1=ALU.mult).then_inc(S["a_done"], 1)

            def act_lo(i, f):
                dve.wait_ge(S["ah_done"], NP * i + f + 1)
                dve.tensor_tensor(al[f][:], ab[f % 2][:], ah[f][:], ALU.subtract).then_inc(S["al_done"], 1)

            def shared_out(i):
                dve.wait_ge(S["d_ps"], NP * (i + 1))
                xi = xs[:, bass.ds(TB * i, TB), :]
                dve.scalar_tensor_tensor(out=xi, in0=bD[:].rearrange("p (t d) -> p t d", t=TB), scalar=1.0 / WS,
                                         in1=xi, op0=ALU.mult, op1=ALU.add).then_inc(S["x2_done"], 1)

            def logits(i):
                dve.wait_ge(S["r_ps"], i + 1)
                dve.tensor_scalar(logit[:], bR[:, 0:TB * E].rearrange("p (t e) -> p t e", e=E), 1.0 / WS, None,
                                  ALU.mult).then_inc(S["logit_done"], 1)
                dve.wait_ge(S["logit_done"], i + 1)
                if not isinstance(i, int) or i >= 1:
                    dve.wait_ge(S["best_done"], 2 * i)
                dve.nop(nofuse=True)
                for t in range(TB):
                    dve.max(top[:, t, :], logit[:, t, :]).then_inc(S["top_done"], 1)
                dve.wait_ge(S["top_done"], TB * (i + 1))
                dve.nop(nofuse=True)
                for t in range(TB):
                    dve.max_index(topi[:, t, :], top[:, t, :], logit[:, t, :]).then_inc(S["topi_done"], 1)
                dve.wait_ge(S["topi_done"], TB * (i + 1))
                for dst, src in ((best, top), (ei, topi)):
                    dve.tensor_copy(dst[:, :, bass.ds(TB * i, TB)], src[:, :, 0:2].rearrange("p t k -> p k t")
                                    ).then_inc(S["best_done"], 1)

            def expert_lo(e, j):
                dve.wait_ge(S["ex_hi"], 3 * e + j + 1)
                part = slice(j * EW // 3, (j + 1) * EW // 3)
                row = lambda w: w[:, bass.ds(e, 1), part].rearrange("p o n -> p (o n)")
                dve.scalar_tensor_tensor(out=row(we_l), in0=stage[:, part], scalar=WS, in1=row(we_h), op0=ALU.mult,
                                         op1=ALU.subtract).then_inc(S["ex_lo"], 1)

            def shared(i, f):
                swiglu(NP * i + f, f % 2)
                act_lo(i, f)

            def step(i, sh, ahead, before=False):
                if before:
                    shared_out(i - 2)
                if ahead:
                    norm(0, i + 1)
                if sh:
                    logits(i - 1)
                if ahead:
                    norm_apply(0, i + 1)
                keys(i)
                queries(i)
                if ahead:
                    split_lo(0, i + 1)
                context_lo(i)
                if sh:
                    shared(i - 1, 0)
                expert_lo(i, 0)
                if sh:
                    shared(i - 1, 1)
                expert_lo(i, 1)
                if sh:
                    shared(i - 1, 2)
                residual(i)
                norm(1, i)
                expert_lo(i, 2)
                norm_apply(1, i)
                if sh:
                    shared(i - 1, 3)
                split_lo(1, i)

            dve.memset(keep[:], 1.0).then_inc(S["const_dve"], 1)
            dve.wait_ge(S["const_dve"], 1)
            dve.memset(keep[:, :, 0:1], 0.0).then_inc(S["const_dve"], 1)
            dve.wait_ge(S["const_pool"], 6)
            dve.tensor_copy(iota_f[:], iota_i[:]).then_inc(S["const_dve"], 1)
            dve.tensor_copy(iota16[:], iota_i[:]).then_inc(S["const_dve"], 1)
            dve.tensor_copy(tok_f[:], tok_i[:]).then_inc(S["const_dve"], 1)
            dve.tensor_copy(full_f[:], full_i[:]).then_inc(S["const_dve"], 1)
            dve.wait_ge(S["x0_in"], 16)
            norm(0, 0)
            norm_apply(0, 0)
            dve.wait_ge(S["att_hi"], 1)
            dve.scalar_tensor_tensor(out=wa_l[:], in0=stage_att, scalar=WS, in1=wa_h[:], op0=ALU.mult,
                                     op1=ALU.subtract).then_inc(S["att_lo"], 1)
            split_lo(0, 0)
            dve.wait_ge(S["bias_in"], 32)
            dve.tensor_scalar(bias1[:], bias[:, 0:2, :], 1.0, None, ALU.add).then_inc(S["bias_done"], 1)
            dve.tensor_scalar(bias_v[:], bias[:, 2, :], WS, None, ALU.mult).then_inc(S["bias_done"], 1)
            dve.wait_ge(S["bias_done"], 2)
            dve.wait_ge(S["x_in"], 16 * (B - 1))
            M = KC * FS
            for m in range(3):
                dve.wait_ge(S["sh_hi"], m + 1)
                dve.scalar_tensor_tensor(out=ws_l[:, m, :], in0=stage_sh[:, m * M:(m + 1) * M], scalar=WS,
                                         in1=ws_h[:, m, :], op0=ALU.mult, op1=ALU.subtract).then_inc(S["sh_lo"], 1)
            dve.wait_ge(S["const_dve"], 6)
            step(0, False, True)
            step(1, True, True)
            with dve.Fori(2, B - 1) as i:
                step(i, True, True, True)
            step(B - 1, True, False, True)
            shared_out(B - 2)
            logits(B - 1)
            dve.wait_ge(S["best_done"], 2 * B)

            n = [0]

            def then(ins):
                n[0] += 1
                ins.then_inc(S["rt"], 1)
                dve.wait_ge(S["rt"], n[0])

            dve.tensor_tensor(sc_d[:], best[:, 1, :], best[:, 0, :], ALU.subtract).then_inc(S["dscore"], 1)
            wide = lambda a: a.rearrange("p (t o) -> p t o", o=1).to_broadcast((P, NT, E))
            for k in range(2):
                then(dve.tensor_tensor(oh[k][:], iota_f[:, 0:E].rearrange("p (o e) -> p o e", o=1).to_broadcast((P, NT, E)),
                                       wide(ei[:, k, :]), ALU.is_equal))
            by_tile = lambda a: a.rearrange("p e t -> p t e")
            dve.tensor_tensor(by_tile(member[:]), oh[0][:], oh[1][:], ALU.add).then_inc(S["member_done"], 1)
            swiglu(NP * (B - 1), 0)
            act_lo(B - 1, 0)
            dve.wait_ge(S["escore"], 1)
            then(dve.tensor_scalar(sc_1[:], sc_e[:], 1.0, None, ALU.add))
            then(dve.reciprocal(score[:, 0, :], sc_1[:]))
            then(dve.tensor_tensor(score[:, 1, :], sc_e[:], score[:, 0, :], ALU.mult))
            flat = lambda a: a.rearrange("p a b -> p (a b)")
            then(dve.tensor_copy(sc16[:], score[:].rearrange("p a b -> p (a b)")))
            then(dve.tensor_copy(vals[:, 1, :], sc16[:]))
            then(dve.tensor_tensor(vals[:, 2, :], score[:].rearrange("p a b -> p (a b)"), vals[:, 1, :], ALU.subtract))
            for k in range(2):
                then(dve.tensor_copy(vals[:, 0, k * NT:(k + 1) * NT], tok_f[:]))
            dve.wait_ge(S["rank_ps"], 1)
            then(dve.tensor_copy(flat(total), bQ[:, P:2 * P]))
            then(dve.tensor_copy(flat(before), bQ[:, 0:P]))
            then(dve.tensor_tensor_scan(flat(run), ones16[:], flat(total), 0.0, ALU.mult, ALU.add))
            then(dve.tensor_reduce(count[:], total, AX.X, ALU.add))
            then(dve.tensor_tensor(cmp, count[:].rearrange("p (e o) -> p e o", o=1).to_broadcast((P, E, NT)),
                                   full_f[:].rearrange("p (o t) -> p o t", o=1).to_broadcast((P, E, NT)), ALU.is_gt))
            then(dve.tensor_reduce(nblk[:], cmp, AX.X, ALU.add))
            then(dve.tensor_tensor_scan(bend[:], ones16[:, 0:E], nblk[:], 0.0, ALU.mult, ALU.add))
            then(dve.tensor_tensor(r1[:], bend[:], nblk[:], ALU.subtract))
            then(dve.tensor_tensor(r2[:], run[:, :, NT - 1], count[:], ALU.subtract))
            then(dve.scalar_tensor_tensor(out=base[:], in0=r1[:], scalar=float(P), in1=r2[:], op0=ALU.mult, op1=ALU.subtract))
            swiglu(NP * (B - 1) + 1, 1)
            act_lo(B - 1, 1)
            then(dve.tensor_tensor(s1, run, total, ALU.subtract))
            then(dve.tensor_tensor(s2, s1, before, ALU.add))
            then(dve.tensor_tensor(s3, s2, base[:].rearrange("p (e o) -> p e o", o=1).to_broadcast((P, E, NT)), ALU.add))
            for k in range(2):
                then(dve.tensor_tensor(pick[k][:], oh[k][:], by_tile(s3), ALU.mult))
                then(dve.tensor_reduce(slot[:, k * NT:(k + 1) * NT], pick[k][:], AX.X, ALU.add))
            then(dve.tensor_copy(slot_i[:], slot[:]))
            then(dve.tensor_scalar(blk_i[:], slot_i[:], 7, None, ALU.arith_shift_right))
            then(dve.tensor_scalar(pos_i[:], slot_i[:], P - 1, None, ALU.bitwise_and))
            then(dve.tensor_copy(blk_f[:], blk_i[:]))
            then(dve.tensor_copy(pos_f[:], pos_i[:]))
            then(dve.tensor_tensor(at_blk[:], iota_f[:, 0:NBP].rearrange("p (o b) -> p o b", o=1).to_broadcast((P, 2 * NT, NBP)),
                                   blk_f[:].rearrange("p (n o) -> p n o", o=1).to_broadcast((P, 2 * NT, NBP)), ALU.is_equal))
            for j in range(3):
                then(dve.tensor_tensor(put[:, :, j, :], at_blk[:],
                                       vals[:, j, :].rearrange("p (n o) -> p n o", o=1).to_broadcast((P, 2 * NT, NBP)), ALU.mult))
            swiglu(NP * (B - 1) + 2, 0)
            act_lo(B - 1, 2)
            for m in range(2 * NT):
                ins = dve.tensor_scalar(at_pos[:, m, :], iota16[:], pos_f[:, m:m + 1], None, ALU.is_equal)
            ins.then_inc(S["put_done"], 1)
            swiglu(NP * (B - 1) + 3, 1)
            act_lo(B - 1, 3)
            then(dve.tensor_tensor(bcmp[:], iota_f[:, 0:NBP].rearrange("p (b o) -> p b o", o=1).to_broadcast((P, NBP, E)),
                                   bend[:].rearrange("p (o e) -> p o e", o=1).to_broadcast((P, NBP, E)), ALU.is_ge))
            then(dve.tensor_reduce(bexp[:], bcmp[:], AX.X, ALU.add))
            then(dve.tensor_scalar(bexp_c[:], bexp[:], float(E - 1), None, ALU.min))
            dve.tensor_copy(blk_expert[:], bexp_c[:]).then_inc(S["bexp_done"], 1)
            shared_out(B - 1)
            dve.wait_ge(S["put_ps"], 1)
            then(dve.tensor_scalar(src_f[:], bV[:, 0:NBP], -1.0, 0.0, ALU.add, ALU.max))
            dve.tensor_copy(src_row[:], src_f[:]).then_inc(S["plan_done"], 1)
            then(dve.tensor_scalar(pad_f[:], bV[:, 0:NBP], 0.0, float(BIG), ALU.is_equal, ALU.mult))
            then(dve.scalar_tensor_tensor(out=dst_f[:], in0=bV[:, 0:NBP], scalar=-1.0, in1=pad_f[:], op0=ALU.add, op1=ALU.add))
            dve.tensor_copy(dst_row[:], dst_f[:]).then_inc(S["plan_done"], 1)
            then(dve.tensor_scalar(slot_lo[:], bV[:, 2 * NBP:3 * NBP], 1.0 / WS, None, ALU.mult))
            dve.scalar_tensor_tensor(out=slot_score[:], in0=bV[:, NBP:2 * NBP], scalar=1.0 / WS, in1=slot_lo[:],
                                     op0=ALU.mult, op1=ALU.add).then_inc(S["plan_done"], 1)
            dve.wait_ge(S["plan_done"], 3)

            def gather_lo(b, q):
                dve.wait_ge(S["gh_done"], b + 1)
                dve.tensor_tensor(gT_l[q].rearrange("p k l -> p (k l)"), bT[:, 0:KC * P],
                                  gT_h[q].rearrange("p k l -> p (k l)"), ALU.subtract).then_inc(S["gl_done"], 1)

            def routed_act_lo(b, q):
                dve.wait_ge(S["ah_done"], NP * B + b + 1)
                dve.tensor_tensor(al[q][:], bK[:], ah[q][:], ALU.subtract).then_inc(S["al_done"], 1)

            def result(b, q):
                dve.wait_ge(S["o_ps"], b + 1)
                if not isinstance(b, int) or b >= 2:
                    dve.wait_ge(S["scattered"], 16 * (b - 1))
                dve.tensor_scalar(ya[q], (bV, bQ)[q][:, 0:D], slot_score[:, bass.ds(b, 1)], None, ALU.mult
                                  ).then_inc(S["y_done"], 1)

            def routed(b, q, first, last):
                if not first:
                    routed_act_lo(b - 1, 1 - q)
                if not last:
                    gather_lo(b + 1, 1 - q)
                swiglu(NP * B + b, q)
                if not first:
                    result(b - 1, 1 - q)

            gather_lo(0, 0)
            routed(0, 0, True, False)
            routed(1, 1, False, False)
            routed(2, 0, False, False)
            with dve.Fori(3, NBLK - 2, 2) as b:
                routed(b, 1, False, False)
                routed(b + 1, 0, False, False)
            routed(NBLK - 2, 1, False, False)
            routed(NBLK - 1, 0, False, True)
            routed_act_lo(NBLK - 1, 0)
            result(NBLK - 1, 0)


def kernel(**inputs):
    import numpy as np
    import concourse.bacc as bacc
    from concourse.bass_utils import run_bass_kernel_spmd

    a = {k: np.asarray(v) for k, v in inputs.items()}

    def rows(w):
        return w.reshape(-1, P, w.shape[-1]).transpose(1, 0, 2).reshape(P, -1)

    att = [rows(a[f"L0_attn_W{m}"].T) for m in "qkvo"] + [rows(a["L0_ffn_router_w"])]
    w1, w2 = a["L0_ffn_w1"], a["L0_ffn_w2"]
    arrays = {
        "x": a["L0_attn_x"],
        "w_att": np.concatenate(att, axis=1),
        "w_bias": np.stack([a[f"L0_attn_b{m}"].reshape(-1, P).T for m in "qkv"], axis=1),
        "w_bo": a["L0_attn_bo"].reshape(1, -1),
        "w_shared": np.stack([rows(a[f"L0_ffn_w_{m}"]) for m in ("gate", "up", "down")], axis=1),
        "w_expert": np.stack([np.concatenate([rows(w1[e]), rows(w2[e])], axis=1) for e in range(w1.shape[0])]),
    }
    arrays = {f"in_{k}": np.ascontiguousarray(v) for k, v in arrays.items()}
    nc = bacc.Bacc("TRN2", target_bir_lowering=False, num_devices=1)
    args = [nc.dram_tensor(k, v.shape, mybir.dt.from_np(v.dtype), kind="ExternalInput").ap() for k, v in arrays.items()]
    out = nc.dram_tensor("out_y", a["L0_attn_x"].shape, F32, kind="ExternalOutput").ap()
    layer_kernel(nc, *args, out)
    r = run_bass_kernel_spmd(nc, [arrays], core_ids=[0])
    return r.results[0]["out_y"]
```

```python
from contextlib import ExitStack

import concourse.bass as bass
from concourse import mybir

ALU = mybir.AluOpType
ACT = mybir.ActivationFunctionType
AX = mybir.AxisListType
F32 = mybir.dt.float32
F16 = mybir.dt.float16
I32 = mybir.dt.int32
U32 = mybir.dt.uint32

P = 128
WS = 64.0
CS = 1.0 / 16.0
EPS = 1e-5


def layer_kernel(nc, x, w_att, w_bias, w_bo, w_shared, w_expert, out):
    B, L, D = x.shape
    NT = B * L // P
    TB = L // P
    KC = D // P
    HEAD_DIM = 16
    SCALE = float(HEAD_DIM) ** -0.5
    E = w_expert.shape[0]
    FS = w_shared.shape[2] // KC
    NP = FS // (2 * P)
    FE = w_expert.shape[2] // (2 * KC + D // P)
    FC = FE // P
    W1 = KC * 2 * FE
    NBLK = (2 * NT * P + E * (P - 1)) // P
    NBP = NBLK + 1
    BIG = 2 * NT * P
    AW = w_att.shape[1]

    scratch = nc.dram_tensor("xn2_rows", (NT * P, D), F32, kind="Internal").ap()
    xv = x.rearrange("b (t p) d -> b p t d", p=P)
    out_rows = out.rearrange("b l d -> (b l) d")
    outv = out.rearrange("b (t p) d -> b p t d", p=P)
    scr_v = scratch.rearrange("(b t p) d -> b p t d", p=P, t=TB)

    with ExitStack() as ctx:
        def sb(name, shape, dt=F32):
            return ctx.enter_context(nc.sbuf_tensor(name, shape, dt))

        def bank(name):
            return ctx.enter_context(nc.psum_tensor(name, [P, 512], F32))

        def sem(name):
            return ctx.enter_context(nc.semaphore(name))

        wa_h, wa_l = sb("wa_h", [P, AW], F16), sb("wa_l", [P, AW], F16)
        ws_h, ws_l = sb("ws_h", [P, 3, KC * FS], F16), sb("ws_l", [P, 3, KC * FS], F16)
        EW = w_expert.shape[2]
        we = sb("we", [P, 2, E, W1], F16)
        wd = sb("wd", [P, E, FC, 2, D], F16)
        stage = sb("stage", [P, EW])
        stage_att = wd[:, E // 2:E, :, :, :].rearrange("p e c s n -> p (e c s n)").bitcast(F32)[:, 0:AW]
        stage_sh = we[:, 1, 2:E, :].rearrange("p e n -> p (e n)").bitcast(F32)[:, 0:3 * KC * FS]

        def att_w(w, m):
            return w[:, m * KC * D:(m + 1) * KC * D].rearrange("p (k n) -> p k n", k=KC)

        def router_w(w):
            return w[:, 4 * KC * D:4 * KC * D + KC * E].rearrange("p (k n) -> p k n", k=KC)

        ident = sb("ident", [P, P])
        tri = sb("tri", [P, P], F16)
        ones16 = sb("ones16", [P, P], F16)
        keep = sb("keep", [P, 2, L], F16)
        minus_half = sb("minus_half", [P, TB])
        iota_i = sb("iota_i", [P, P], I32)
        iota_f = sb("iota_f", [P, P])
        iota16 = sb("iota16", [P, P], F16)
        tok_i = sb("tok_i", [P, NT], I32)
        tok_f = sb("tok_f", [P, NT])
        full_i = sb("full_i", [P, NT], I32)
        full_f = sb("full_f", [P, NT])

        xs = sb("xs", [P, NT, D])
        bias = sb("bias", [P, 3, KC])
        bias1 = sb("bias1", [P, 2, KC])
        bias_v = sb("bias_v", [P, KC])
        bo = sb("bo", [P, D])
        st = [sb(f"st{n}", [P, TB, 6]) for n in range(2)]
        mv = [sb(f"mv{n}", [P, TB, 2]) for n in range(2)]
        ve = [sb(f"ve{n}", [P, TB]) for n in range(2)]
        y0 = [sb(f"y0{n}", [P, TB]) for n in range(2)]
        nt_ = [sb(f"nt{n}", [P, TB]) for n in range(2)]
        nu = [sb(f"nu{n}", [P, TB]) for n in range(2)]
        rstd = [sb(f"rstd{n}", [P, TB]) for n in range(2)]
        xn = [sb(f"xn{n}", [P, TB, D]) for n in range(2)]
        xT_h = [sb(f"xTh{n}", [P, KC, L], F16) for n in range(2)]
        xT_l = [sb(f"xTl{n}", [P, KC, L], F16) for n in range(2)]
        work = sb("work", [P, 5, KC, L])
        ek, rk, eq, rq, kvs = (work[:, n, :, :] for n in range(5))
        phik, kv, phiq, cx = ek, rk, eq, rq
        cx_h, cx_l = sb("cx_h", [P, KC, L], F16), sb("cx_l", [P, KC, L], F16)
        sg = [sb(f"sg{n}", [P, 512]) for n in range(2)]
        ab = [sb(f"ab{n}", [P, 512]) for n in range(2)]
        ah = [sb(f"ah{n}", [P, 512], F16) for n in range(NP)]
        al = [sb(f"al{n}", [P, 512], F16) for n in range(NP)]

        logit = sb("logit", [P, TB, E])
        top = sb("top", [P, TB, 8])
        topi = sb("topi", [P, TB, 8], U32)
        best = sb("best", [P, 2, NT])
        ei = sb("ei", [P, 2, NT])
        sc_d, sc_e, sc_1 = sb("sc_d", [P, NT]), sb("sc_e", [P, NT]), sb("sc_1", [P, NT])
        score = sb("score", [P, 2, NT])
        oh = [sb(f"oh{k}", [P, NT, E]) for k in range(2)]
        member = sb("member", [P, E, NT], F16)
        by_expert = lambda a: a.rearrange("p (e t) -> p e t", e=E)
        before, total, run, cmp = (by_expert(xn[0][:, n // 2, (n % 2) * P:(n % 2 + 1) * P]) for n in range(4))
        s1, s2 = (by_expert(xT_h[0][:, n, :].bitcast(F32)) for n in range(2))
        s3 = by_expert(xT_l[0][:, 0, :].bitcast(F32))
        count, nblk, bend = sb("count", [P, E]), sb("nblk", [P, E]), sb("bend", [P, E])
        r1, r2, base = sb("r1", [P, E]), sb("r2", [P, E]), sb("base", [P, E])
        pick = [sb(f"pick{k}", [P, NT, E]) for k in range(2)]
        slot = sb("slot", [P, 2 * NT])
        slot_i, blk_i, pos_i = (sb(n, [P, 2 * NT], I32) for n in ("slot_i", "blk_i", "pos_i"))
        blk_f, pos_f = sb("blk_f", [P, 2 * NT]), sb("pos_f", [P, 2 * NT])
        sc16 = sb("sc16", [P, 2 * NT], F16)
        vals = sb("vals", [P, 3, 2 * NT])
        at_pos = stage[:].bitcast(F16)[:, 0:2 * NT * P].rearrange("p (n q) -> p n q", n=2 * NT)
        work16 = work[:].rearrange("p a k l -> p (a k l)").bitcast(F16)
        put = work16[:, 0:6 * NT * NBP].rearrange("p (n a b) -> p n a b", a=3, b=NBP)
        at_blk = work16[:, 6 * NT * NBP:8 * NT * NBP].rearrange("p (n b) -> p n b", b=NBP)
        bcmp = sb("bcmp", [P, NBP, E])
        bexp, bexp_c = sb("bexp", [P, NBP]), sb("bexp_c", [P, NBP])
        blk_expert = sb("blk_expert", [P, NBP], I32)
        src_f, pad_f, dst_f = sb("src_f", [P, NBP]), sb("pad_f", [P, NBP]), sb("dst_f", [P, NBP])
        src_row, dst_row = sb("src_row", [P, NBP], U32), sb("dst_row", [P, NBP], U32)
        slot_lo, slot_score = sb("slot_lo", [P, NBP]), sb("slot_score", [P, NBP])

        gi = [sb(f"gi{n}", [P, 1], U32) for n in range(2)]
        si = [sb(f"si{n}", [P, 1], U32) for n in range(2)]
        xg = [sb(f"xg{n}", [P, D]) for n in range(2)]
        gT_h = [cx_h[:, n, :].rearrange("p (k l) -> p k l", k=KC) for n in range(2)]
        gT_l = [cx_l[:, n, :].rearrange("p (k l) -> p k l", k=KC) for n in range(2)]
        ya = [xn[1][:, n, :] for n in range(2)]
        yl = [xn[0][:, n, :] for n in range(2)]

        bT, bK, bV, bQ, bG, bU, bD, bR = (bank(n) for n in ("bT", "bK", "bV", "bQ", "bG", "bU", "bD", "bR"))

        names = """x0_in x1_in x_in att_k_in att_k_hi att_k_lo att_in bias_in sh_in ex_in att_hi att_lo sh_hi sh_lo ex_hi ex_lo
            const_pool const_dve bias_done xn2_saved out_saved
            ln1_step ln2_step ve1 ve2 pow1 pow2 xn1 xn2 xbo
            t1 t1_hi t1_lo t2 t2_hi t2_lo k_ps v_ps q_ps ek_done rk_done eq_done rq_done
            phik_done kv_done kvs_done phiq_done cx_done cxh_done cxl_done wo_ps x1_done
            g_ps u_ps sg_done a_done ah_done al_done d_ps x2_done
            r_ps logit_done top_done topi_done best_done
            rt dscore escore member_done rank_ps put_done put_ps plan_done bexp_done
            gi_done gathered0 gathered1 tx_ps gh_done gl_done ta_ps o_ps yl_done y_done si_done scattered""".split()
        S = {n: sem(n) for n in names}

        block = ctx.enter_context(nc.Block())

        def product(pe, dst, lhs_h, lhs_l, rhs_h, rhs_l, n, first=True, last=True, lone=False):
            steps = [(lhs_h, rhs_h), (lhs_h, rhs_l), (lhs_l, rhs_h)]
            for s, (a, b) in enumerate(steps):
                for c in range(n):
                    ins = pe.matmul(dst, a(c), b(c), start=first and s == 0 and c == 0,
                                    stop=last and s == 2 and c == n - 1, skip_group_check=lone)
            return ins

        def expert_part(e, j, lo):
            if j < 2:
                half = slice(j * W1 // 2, (j + 1) * W1 // 2)
                return we[:, lo, bass.ds(e, 1), half].rearrange("p o n -> p (o n)"), stage[:, half]
            return (wd[:, bass.ds(e, 1), :, lo, :].rearrange("p o c n -> p (o c) n"),
                    stage[:, W1:EW].rearrange("p (c n) -> p c n", n=D))

        @block.sync
        def _(sp):
            sp.dma_start(xs[:, 0:TB, :], xv[0]).then_inc(S["x0_in"], 16)
            sp.dma_start(stage_att[:, 0:KC * D], w_att[:, 0:KC * D]).then_inc(S["att_k_in"], 16)
            sp.dma_start(stage_att[:, KC * D:AW], w_att[:, KC * D:AW]).then_inc(S["att_in"], 16)
            sp.dma_start(bias[:], w_bias).then_inc(S["bias_in"], 16)
            sp.dma_start(bo[:], w_bo.to_broadcast((P, D))).then_inc(S["bias_in"], 16)
            sp.dma_start(xs[:, TB:2 * TB, :], xv[1]).then_inc(S["x1_in"], 16)
            sp.dma_start(stage_sh, w_shared.rearrange("p m n -> p (m n)")).then_inc(S["sh_in"], 16)
            sp.dma_start(xs[:, 2 * TB:NT, :].rearrange("p (b t) d -> p b t d", t=TB),
                         x[2:B].rearrange("b (t p) d -> p b t d", p=P)).then_inc(S["x_in"], 16)
            sp.dma_start(stage[:], w_expert[0]).then_inc(S["ex_in"], 16)

            def step(i, last):
                sp.wait_ge(S["xn2"], TB * (i + 1))
                sp.dma_start(scr_v[i] if isinstance(i, int) else scr_v[bass.ds(i, 1)].rearrange("o p t d -> (o p) t d"),
                             xn[1][:]).then_inc(S["xn2_saved"], 16)
                if not last:
                    sp.wait_ge(S["ex_hi"], 3 * (i + 1))
                    sp.wait_ge(S["ex_lo"], 3 * (i + 1))
                    src = w_expert[i + 1] if isinstance(i, int) else \
                        w_expert[bass.ds(i + 1, 1)].rearrange("o p n -> (o p) n")
                    sp.dma_start(stage[:], src).then_inc(S["ex_in"], 16)

            def save(i):
                sp.wait_ge(S["x2_done"], i + 1)
                dst = outv[i] if isinstance(i, int) else outv[bass.ds(i, 1)].rearrange("o p t d -> (o p) t d")
                sp.dma_start(dst, xs[:, bass.ds(TB * i, TB), :]).then_inc(S["out_saved"], 16)

            step(0, False)
            step(1, False)
            with sp.Fori(2, B - 1) as i:
                save(i - 2)
                step(i, False)
            save(B - 3)
            step(B - 1, True)
            save(B - 2)
            save(B - 1)
            sp.wait_ge(S["out_saved"], 16 * B)
            sp.wait_ge(S["scattered"], 16 * NBLK)

        @block.gpsimd
        def _(pool):
            pool.memset(ident[:], 0.0).then_inc(S["const_pool"], 1)
            pool.memset(ones16[:], 1.0).then_inc(S["const_pool"], 1)
            pool.memset(minus_half[:], -0.5).then_inc(S["const_pool"], 1)
            pool.iota(iota_i[:], pattern=[[1, P]], base=0, channel_multiplier=0).then_inc(S["const_pool"], 1)
            pool.iota(tok_i[:], pattern=[[P, NT]], base=1, channel_multiplier=1).then_inc(S["const_pool"], 1)
            pool.iota(full_i[:], pattern=[[P, NT]], base=0, channel_multiplier=0).then_inc(S["const_pool"], 1)
            pool.wait_ge(S["const_pool"], 6)
            pool.affine_select(out=ident[:], in_=ident[:], compare_op=ALU.not_equal, fill=1.0, base=0,
                               pattern=[[-1, P]], channel_multiplier=1).then_inc(S["const_pool"], 1)
            pool.affine_select(out=tri[:], in_=ones16[:], compare_op=ALU.is_ge, fill=0.0, base=-1,
                               pattern=[[1, P]], channel_multiplier=-1).then_inc(S["const_pool"], 1)

            def rsqrt(n, i):
                pool.wait_ge(S[f"ve{n + 1}"], i + 1)
                pool.tensor_tensor(y0[n][:], ve[n][:], minus_half[:], ALU.pow).then_inc(S[f"pow{n + 1}"], 1)

            def add_bo(i):
                pool.wait_ge(S["xn1"], TB * (i + 1))
                xi = xs[:, bass.ds(TB * i, TB), :]
                pool.tensor_tensor(xi, xi, bo[:].rearrange("p (o d) -> p o d", o=1).to_broadcast((P, TB, D)),
                                   ALU.add).then_inc(S["xbo"], 1)

            rsqrt(0, 0)
            pool.wait_ge(S["bias_in"], 32)
            add_bo(0)
            with pool.Fori(0, B - 1) as i:
                rsqrt(0, i + 1)
                add_bo(i + 1)
                rsqrt(1, i)
            rsqrt(1, B - 1)

            pool.wait_ge(S["plan_done"], 3)
            pool.wait_ge(S["xn2_saved"], 16 * B)

            def gather(b, q, fresh):
                if not fresh:
                    pool.wait_ge(S["tx_ps"], b - 1)
                pool.tensor_copy(gi[q][:], src_row[:, bass.ds(b, 1)]).then_inc(S["gi_done"], 1)
                pool.wait_ge(S["gi_done"], b + 1)
                pool.nop(nofuse=True)
                pool.indirect_dma_start(xg[q][:], None, scratch, bass.IndirectOffsetOnAxis(ap=gi[q][:], axis=0)
                                        ).then_inc(S[f"gathered{q}"], 16)

            def scatter(b, q):
                if not isinstance(b, int) or b >= 1:
                    pool.wait_ge(S["scattered"], 16 * b)
                pool.tensor_copy(si[q][:], dst_row[:, bass.ds(b, 1)]).then_inc(S["si_done"], 1)
                pool.wait_ge(S["si_done"], b + 1)
                pool.wait_ge(S["y_done"], b + 1)
                pool.nop(nofuse=True)
                pool.indirect_dma_start(out_rows, bass.IndirectOffsetOnAxis(ap=si[q][:], axis=0), ya[q], None,
                                        bounds_check=NT * P - 1, oob_is_err=False, compute_op=ALU.add
                                        ).then_inc(S["scattered"], 16)

            for b in range(4):
                gather(b, b % 2, b < 2)
            pool.wait_ge(S["out_saved"], 16 * B)
            gather(4, 0, False)
            scatter(0, 0)
            with pool.Fori(1, NBLK - 4, 2) as b:
                for q in range(2):
                    gather(b + 4 + q, 1 - q, False)
                    scatter(b + q, 1 - q)
            for b in range(NBLK - 4, NBLK):
                scatter(b, b % 2)

        @block.tensor
        def _(pe):
            def norm_T(n, i):
                pe.wait_ge(S[f"xn{n + 1}"], TB * (i + 1))
                if n == 0:
                    if not isinstance(i, int) or i >= 2:
                        pe.wait_ge(S["t2_lo"], i - 1)
                    if not isinstance(i, int) or i >= 1:
                        pe.wait_ge(S["t1_lo"], i)
                else:
                    pe.wait_ge(S["t1_lo"], i + 1 if isinstance(i, int) and i == B - 1 else i + 2)
                for t in range(TB):
                    for k in range(KC):
                        ins = pe.transpose(bT[:, k * L + t * P:k * L + (t + 1) * P],
                                           xn[n][:, t, k * P:(k + 1) * P], ident[:])
                ins.then_inc(S[f"t{n + 1}"], 1)

            def project(i):
                pe.wait_ge(S["t1_lo"], i + 1)
                for m, dst, done in ((0, bK, "k_ps"), (1, bQ, "q_ps"), (2, bV, "v_ps")):
                    if not isinstance(i, int) or i >= 1:
                        if m == 0:
                            pe.wait_ge(S["x1_done"], i)
                        elif m == 1:
                            pe.wait_ge(S["rq_done"], KC * i)
                        else:
                            pe.wait_ge(S["kv_done"], KC * i)
                    elif m == 1:
                        pe.wait_ge(S["att_lo"], 1)
                    wh, wl = att_w(wa_h, m), att_w(wa_l, m)
                    for c in range(KC):
                        ins = product(pe, dst[:, c * L:(c + 1) * L],
                                      lambda k: wh[:, k, c * P:(c + 1) * P], lambda k: wl[:, k, c * P:(c + 1) * P],
                                      lambda k: xT_h[0][:, k, :], lambda k: xT_l[0][:, k, :], KC)
                    ins.then_inc(S[done], 1)

            def attend_out(i):
                pe.wait_ge(S["cxl_done"], i + 1)
                wh, wl = att_w(wa_h, 3), att_w(wa_l, 3)
                for t in range(TB):
                    ins = product(pe, bK[:, t * D:(t + 1) * D],
                                  lambda k: cx_h[:, k, t * P:(t + 1) * P], lambda k: cx_l[:, k, t * P:(t + 1) * P],
                                  lambda k: wh[:, k, :], lambda k: wl[:, k, :], KC)
                ins.then_inc(S["wo_ps"], 1)

            def route(i):
                pe.wait_ge(S["t2_lo"], i + 1)
                if not isinstance(i, int) or i >= 1:
                    pe.wait_ge(S["logit_done"], i)
                wh, wl = router_w(wa_h), router_w(wa_l)
                for t in range(TB):
                    ins = product(pe, bR[:, t * E:(t + 1) * E],
                                  lambda k: xT_h[1][:, k, t * P:(t + 1) * P], lambda k: xT_l[1][:, k, t * P:(t + 1) * P],
                                  lambda k: wh[:, k, :], lambda k: wl[:, k, :], KC)
                ins.then_inc(S["r_ps"], 1)

            def gate_up(i, f):
                n = NP * i + f
                for m, dst, done, free in ((0, bG, "g_ps", "sg_done"), (1, bU, "u_ps", "a_done")):
                    if not isinstance(i, int) or n >= 1:
                        pe.wait_ge(S[free], n)
                    wh = ws_h[:, m, :].rearrange("p (k n) -> p k n", k=KC)
                    wl = ws_l[:, m, :].rearrange("p (k n) -> p k n", k=KC)
                    for c in range(2):
                        at = (2 * f + c) * P
                        ins = product(pe, dst[:, c * L:(c + 1) * L],
                                      lambda k: wh[:, k, at:at + P], lambda k: wl[:, k, at:at + P],
                                      lambda k: xT_h[1][:, k, :], lambda k: xT_l[1][:, k, :], KC)
                    ins.then_inc(S[done], 1)

            def down(i, f):
                pe.wait_ge(S["al_done"], NP * i + f + 1)
                if f == 0 and (not isinstance(i, int) or i >= 1):
                    pe.wait_ge(S["x2_done"], i)
                wh = ws_h[:, 2, :].rearrange("p (c n) -> p c n", n=D)
                wl = ws_l[:, 2, :].rearrange("p (c n) -> p c n", n=D)
                for t in range(TB):
                    ins = product(pe, bD[:, t * D:(t + 1) * D],
                                  lambda c: ah[f][:, c * L + t * P:c * L + (t + 1) * P],
                                  lambda c: al[f][:, c * L + t * P:c * L + (t + 1) * P],
                                  lambda c: wh[:, 2 * f + c, :], lambda c: wl[:, 2 * f + c, :], 2,
                                  first=(f == 0 and t == 0), last=(f == NP - 1), lone=True)
                ins.then_inc(S["d_ps"], 1)

            def step(i, shared, ahead):
                project(i)
                if shared:
                    route(i - 1)
                    if isinstance(i, int) and i == 1:
                        pe.wait_ge(S["sh_lo"], 2)
                    gate_up(i - 1, 0)
                    gate_up(i - 1, 1)
                    if isinstance(i, int) and i == 1:
                        pe.wait_ge(S["sh_lo"], 3)
                    down(i - 1, 0)
                attend_out(i)
                if shared:
                    gate_up(i - 1, 2)
                if ahead:
                    norm_T(0, i + 1)
                if shared:
                    gate_up(i - 1, 3)
                    down(i - 1, 1)
                norm_T(1, i)
                if shared:
                    down(i - 1, 2)
                    down(i - 1, 3)

            pe.wait_ge(S["const_pool"], 8)
            norm_T(0, 0)
            pe.wait_ge(S["att_k_lo"], 1)
            step(0, False, True)
            step(1, True, True)
            with pe.Fori(2, B - 1) as i:
                step(i, True, True)
            step(B - 1, True, False)
            route(B - 1)
            gate_up(B - 1, 0)
            gate_up(B - 1, 1)
            down(B - 1, 0)
            pe.wait_ge(S["member_done"], 1)
            pe.wait_ge(S["eq_done"], KC * B)
            pe.wait_ge(S["rq_done"], KC * B)
            mem = member[:].rearrange("p e t -> p (e t)")
            pe.matmul(bQ[:, 0:P], tri[:], mem, start=True, stop=True)
            pe.matmul(bQ[:, P:2 * P], ones16[:], mem, start=True, stop=True).then_inc(S["rank_ps"], 1)
            gate_up(B - 1, 2)
            down(B - 1, 1)
            gate_up(B - 1, 3)
            down(B - 1, 2)
            down(B - 1, 3)
            pe.wait_ge(S["put_done"], 1)
            for n in range(2 * NT):
                ins = pe.matmul(bV[:, 0:3 * NBP], at_pos[:, n, :], put[:, n, :, :].rearrange("p a b -> p (a b)"),
                                start=(n == 0), stop=(n == 2 * NT - 1))
            ins.then_inc(S["put_ps"], 1)

            def turn_x(b, q):
                pe.wait_ge(S[f"gathered{q}"], 8 * (b - q) + 16)
                for k in range(KC):
                    ins = pe.transpose(bT[:, k * P:(k + 1) * P], xg[q][:, k * P:(k + 1) * P], ident[:])
                ins.then_inc(S["tx_ps"], 1)

            def turn_a(b, q):
                pe.wait_ge(S["a_done"], NP * B + b + 1)
                for c in range(FC):
                    ins = pe.transpose(bK[:, c * P:(c + 1) * P], ab[q][:, c * P:(c + 1) * P], ident[:])
                ins.then_inc(S["ta_ps"], 1)

            def expert_up(b, q, e, half):
                dst, done = ((bG, "g_ps"), (bU, "u_ps"))[half]
                if half == 0:
                    pe.wait_ge(S["gl_done"], b + 1)
                w = [we[:, lo, bass.ds(e, 1), :].rearrange("p o (k h n) -> p (o k) h n", k=KC, h=2) for lo in range(2)]
                product(pe, dst[:], lambda k: gT_h[q][:, k, :], lambda k: gT_l[q][:, k, :],
                        lambda k: w[0][:, k, half, :], lambda k: w[1][:, k, half, :], KC).then_inc(S[done], 1)

            def expert_down(b, q, e):
                pe.wait_ge(S["al_done"], NP * B + b + 1)
                w = wd[:, bass.ds(e, 1), :, :, :].rearrange("p o c s n -> p (o c) (s n)")
                dst = (bV, bQ)[q]
                for c in range(FC):
                    pe.matmul(dst[:], ah[q][:, c * P:(c + 1) * P], w[:, c, :], start=(c == 0), stop=False,
                              skip_group_check=True)
                for c in range(FC):
                    ins = pe.matmul(dst[:, 0:D], al[q][:, c * P:(c + 1) * P], w[:, c, 0:D], start=False,
                                    stop=(c == FC - 1), skip_group_check=True)
                ins.then_inc(S["o_ps"], 1)

            expert_reg = [pe.alloc_register(f"expert_reg{q}") for q in range(2)]

            def load_expert(b, q):
                pe.reg_load(expert_reg[q], blk_expert[0:1, bass.ds(b, 1)])

            def expert(q):
                return pe.snap(expert_reg[q], min_val=0, max_val=E - 1)

            def routed(b, q, first, last):
                e = expert(q)
                expert_up(b, q, e, 0)
                if not first:
                    turn_a(b - 1, 1 - q)
                if not last:
                    turn_x(b + 1, 1 - q)
                expert_up(b, q, e, 1)
                if not first:
                    expert_down(b - 1, 1 - q, expert(1 - q))
                if not last:
                    load_expert(b + 1, 1 - q)

            pe.wait_ge(S["bexp_done"], 1)
            pe.wait_ge(S["ex_hi"], 3 * E)
            pe.wait_ge(S["ex_lo"], 3 * E)
            pe.wait_ge(S["plan_done"], 3)
            pe.wait_ge(S["t2_lo"], B)
            pe.wait_ge(S["x1_done"], B)
            load_expert(0, 0)
            turn_x(0, 0)
            routed(0, 0, True, False)
            routed(1, 1, False, False)
            routed(2, 0, False, False)
            with pe.Fori(3, NBLK - 2, 2) as b:
                routed(b, 1, False, False)
                routed(b + 1, 0, False, False)
            routed(NBLK - 2, 1, False, False)
            routed(NBLK - 1, 0, False, True)
            turn_a(NBLK - 1, 0)
            expert_down(NBLK - 1, 0, expert(0))

        @block.scalar
        def _(act):
            def split_hi(n, i):
                act.wait_ge(S[f"t{n + 1}"], i + 1)
                if not isinstance(i, int) or i >= 1:
                    if n == 0:
                        act.wait_ge(S["v_ps"], i)
                    else:
                        act.wait_ge(S["r_ps"], i)
                        act.wait_ge(S["u_ps"], NP * i)
                act.activation(xT_h[n][:].rearrange("p k l -> p (k l)"), bT[:], ACT.Copy).then_inc(S[f"t{n + 1}_hi"], 1)

            def exps(i):
                for src, ready, e, r, m, ed, rd, used in ((bK, "k_ps", ek, rk, 1, "ek_done", "rk_done", "kvs_done"),
                                                          (bQ, "q_ps", eq, rq, 0, "eq_done", "rq_done", "cxl_done")):
                    act.wait_ge(S[ready], i + 1)
                    if not isinstance(i, int) or i >= 1:
                        act.wait_ge(S[used], i)
                    for c in range(KC):
                        act.activation(e[:, c, :], src[:, c * L:(c + 1) * L], ACT.Exp, bias=bias[:, m, c:c + 1],
                                       scale=1.0 / WS).then_inc(S[ed], 1)
                    for c in range(KC):
                        act.activation(r[:, c, :], src[:, c * L:(c + 1) * L], ACT.Identity, bias=bias1[:, m, c:c + 1],
                                       scale=1.0 / WS).then_inc(S[rd], 1)

            def context_hi(i):
                act.wait_ge(S["cx_done"], i + 1)
                if not isinstance(i, int) or i >= 1:
                    act.wait_ge(S["wo_ps"], i)
                act.activation(cx_h[:], cx, ACT.Copy).then_inc(S["cxh_done"], 1)

            def silu(n, q):
                act.wait_ge(S["g_ps"], n + 1)
                act.wait_ge(S["a_done"], n)
                act.activation(sg[q][:], bG[:], ACT.Silu, scale=1.0 / WS).then_inc(S["sg_done"], 1)

            def act_hi(i, f):
                n = NP * i + f
                act.wait_ge(S["a_done"], n + 1)
                if not isinstance(i, int) or i >= 1:
                    act.wait_ge(S["d_ps"], n - NP + 1)
                act.activation(ah[f][:], ab[f % 2][:], ACT.Copy).then_inc(S["ah_done"], 1)

            def expert_hi(e, j):
                if j == 0:
                    act.wait_ge(S["ex_in"], 16 * (e + 1))
                    if isinstance(e, int) and e == E // 2:
                        act.wait_ge(S["sh_lo"], 3)
                dst, src = expert_part(e, j, 0)
                act.activation(dst, src, ACT.Copy, scale=WS).then_inc(S["ex_hi"], 1)

            def shared(i, f):
                silu(NP * i + f, f % 2)
                act_hi(i, f)

            def step(i, sh, ahead):
                exps(i)
                if sh:
                    silu(NP * (i - 1), 0)
                context_hi(i)
                if sh:
                    act_hi(i - 1, 0)
                    silu(NP * (i - 1) + 1, 1)
                else:
                    M = KC * FS
                    act.wait_ge(S["sh_in"], 16)
                    for m in range(2):
                        act.activation(ws_h[:, m, :], stage_sh[:, m * M:(m + 1) * M], ACT.Copy, scale=WS
                                       ).then_inc(S["sh_hi"], 1)
                    split_hi(0, i + 1)
                    act.activation(ws_h[:, 2, :], stage_sh[:, 2 * M:3 * M], ACT.Copy, scale=WS).then_inc(S["sh_hi"], 1)
                    split_hi(1, i)
                expert_hi(i, 0)
                if sh:
                    act_hi(i - 1, 1)
                expert_hi(i, 1)
                if sh:
                    silu(NP * (i - 1) + 2, 0)
                    if ahead:
                        split_hi(0, i + 1)
                    act_hi(i - 1, 2)
                    silu(NP * (i - 1) + 3, 1)
                expert_hi(i, 2)
                if sh:
                    act_hi(i - 1, 3)
                    split_hi(1, i)

            act.wait_ge(S["att_k_in"], 16)
            act.activation(wa_h[:, 0:KC * D], stage_att[:, 0:KC * D], ACT.Copy, scale=WS).then_inc(S["att_k_hi"], 1)
            split_hi(0, 0)
            act.wait_ge(S["att_in"], 16)
            act.activation(wa_h[:, KC * D:AW], stage_att[:, KC * D:AW], ACT.Copy, scale=WS).then_inc(S["att_hi"], 1)
            act.wait_ge(S["bias_done"], 2)
            step(0, False, True)
            step(1, True, True)
            with act.Fori(2, B - 1) as i:
                step(i, True, True)
            step(B - 1, True, False)
            shared(B - 1, 0)
            act.wait_ge(S["dscore"], 1)
            act.activation(sc_e[:], sc_d[:], ACT.Exp).then_inc(S["escore"], 1)
            for f in range(1, NP):
                shared(B - 1, f)

            def gather_hi(b, q):
                act.wait_ge(S["tx_ps"], b + 1)
                if not isinstance(b, int) or b >= 2:
                    act.wait_ge(S["u_ps"], NP * B + b - 1)
                act.activation(gT_h[q].rearrange("p k l -> p (k l)"), bT[:, 0:KC * P], ACT.Copy).then_inc(S["gh_done"], 1)

            def routed_act_hi(b, q):
                act.wait_ge(S["ta_ps"], b + 1)
                if isinstance(b, int) and b < 2:
                    act.wait_ge(S["d_ps"], NP * B)
                else:
                    act.wait_ge(S["o_ps"], b - 1)
                act.activation(ah[q][:], bK[:], ACT.Copy).then_inc(S["ah_done"], 1)

            def result_lo(b, q):
                act.wait_ge(S["o_ps"], b + 1)
                if not isinstance(b, int) or b >= 2:
                    act.wait_ge(S["y_done"], b - 1)
                act.activation(yl[q], (bV, bQ)[q][:, D:2 * D], ACT.Copy, scale=slot_score[:, bass.ds(b, 1)]
                               ).then_inc(S["yl_done"], 1)

            def routed(b, q, first, last):
                silu(NP * B + b, q)
                if not first:
                    routed_act_hi(b - 1, 1 - q)
                if not last:
                    gather_hi(b + 1, 1 - q)
                if not first:
                    result_lo(b - 1, 1 - q)

            gather_hi(0, 0)
            routed(0, 0, True, False)
            routed(1, 1, False, False)
            routed(2, 0, False, False)
            with act.Fori(3, NBLK - 2, 2) as b:
                routed(b, 1, False, False)
                routed(b + 1, 0, False, False)
            routed(NBLK - 2, 1, False, False)
            routed(NBLK - 1, 0, False, True)
            routed_act_hi(NBLK - 1, 0)
            result_lo(NBLK - 1, 0)

        @block.vector
        def _(dve):
            LN = 7

            def norm(n, i):
                s = S[f"ln{n + 1}_step"]
                at = LN * i
                for t in range(TB):
                    dve.bn_stats(st[n][:, t, :], xs[:, bass.ds(TB * i + t, 1), :].rearrange("p o d -> p (o d)")).then_inc(s, 1)
                dve.wait_ge(s, at + 2)
                dve.nop(nofuse=True)
                for t in range(TB):
                    dve.bn_aggr(mv[n][:, t, :], st[n][:, t, :]).then_inc(s, 1)
                dve.wait_ge(s, at + 4)
                dve.tensor_scalar(ve[n][:], mv[n][:, :, 1], EPS, None, ALU.add).then_inc(S[f"ve{n + 1}"], 1)

            def norm_apply(n, i):
                s = S[f"ln{n + 1}_step"]
                at = LN * i
                dve.wait_ge(S[f"pow{n + 1}"], i + 1)
                dve.tensor_tensor(nt_[n][:], y0[n][:], y0[n][:], ALU.mult).then_inc(s, 1)
                dve.wait_ge(s, at + 5)
                dve.scalar_tensor_tensor(out=nu[n][:], in0=nt_[n][:], scalar=-0.5, in1=ve[n][:], op0=ALU.mult,
                                         op1=ALU.mult).then_inc(s, 1)
                dve.wait_ge(s, at + 6)
                dve.scalar_tensor_tensor(out=rstd[n][:], in0=nu[n][:], scalar=1.5, in1=y0[n][:], op0=ALU.add,
                                         op1=ALU.mult).then_inc(s, 1)
                dve.wait_ge(s, at + 7)
                if not isinstance(i, int) or i >= 1:
                    dve.wait_ge(S[f"t{n + 1}"], i)
                    if n == 1:
                        dve.wait_ge(S["xn2_saved"], 16 * i)
                for t in range(TB):
                    dve.tensor_scalar(xn[n][:, t, :], xs[:, bass.ds(TB * i + t, 1), :].rearrange("p o d -> p (o d)"),
                                      mv[n][:, t, 0:1], rstd[n][:, t:t + 1], ALU.subtract, ALU.mult
                                      ).then_inc(S[f"xn{n + 1}"], 1)

            def split_lo(n, i):
                dve.wait_ge(S[f"t{n + 1}_hi"], i + 1)
                dve.tensor_tensor(xT_l[n][:].rearrange("p k l -> p (k l)"), bT[:],
                                  xT_h[n][:].rearrange("p k l -> p (k l)"), ALU.subtract).then_inc(S[f"t{n + 1}_lo"], 1)

            def keys(i):
                dve.wait_ge(S["ek_done"], KC * (i + 1))
                dve.wait_ge(S["rk_done"], KC * (i + 1))
                dve.scalar_tensor_tensor(out=phik, in0=ek, scalar=1.0, in1=rk, op0=ALU.min, op1=ALU.max
                                         ).then_inc(S["phik_done"], 1)
                dve.wait_ge(S["phik_done"], i + 1)
                dve.wait_ge(S["v_ps"], i + 1)
                for c in range(KC):
                    dve.scalar_tensor_tensor(out=kv[:, c, :], in0=bV[:, c * L:(c + 1) * L], scalar=bias_v[:, c:c + 1],
                                             in1=phik[:, c, :], op0=ALU.add, op1=ALU.mult).then_inc(S["kv_done"], 1)

            def sums(i):
                dve.wait_ge(S["kv_done"], KC * (i + 1))
                dve.tensor_tensor_scan(kvs.rearrange("p k l -> p (k l)"), keep[:].rearrange("p k l -> p (k l)"),
                                       kv.rearrange("p k l -> p (k l)"), 0.0, ALU.mult, ALU.add
                                       ).then_inc(S["kvs_done"], 1)

            def queries(i):
                dve.wait_ge(S["eq_done"], KC * (i + 1))
                dve.wait_ge(S["rq_done"], KC * (i + 1))
                dve.scalar_tensor_tensor(out=phiq, in0=eq, scalar=1.0, in1=rq, op0=ALU.min, op1=ALU.max
                                         ).then_inc(S["phiq_done"], 1)

            def context(i):
                dve.wait_ge(S["phiq_done"], i + 1)
                dve.wait_ge(S["kvs_done"], i + 1)
                if not isinstance(i, int) or i >= 1:
                    dve.wait_ge(S["cxh_done"], i)
                dve.scalar_tensor_tensor(out=cx, in0=kvs, scalar=SCALE * CS / WS, in1=phiq, op0=ALU.mult,
                                         op1=ALU.mult).then_inc(S["cx_done"], 1)

            def context_lo(i):
                dve.wait_ge(S["cxh_done"], i + 1)
                dve.tensor_tensor(cx_l[:], cx, cx_h[:], ALU.subtract).then_inc(S["cxl_done"], 1)

            def residual(i):
                dve.wait_ge(S["wo_ps"], i + 1)
                dve.wait_ge(S["xbo"], i + 1)
                xi = xs[:, bass.ds(TB * i, TB), :]
                dve.scalar_tensor_tensor(out=xi, in0=bK[:].rearrange("p (t d) -> p t d", t=TB), scalar=1.0 / (WS * CS),
                                         in1=xi, op0=ALU.mult, op1=ALU.add).then_inc(S["x1_done"], 1)
                dve.wait_ge(S["x1_done"], i + 1)
                dve.nop(nofuse=True)

            def swiglu(n, q):
                dve.wait_ge(S["sg_done"], n + 1)
                dve.wait_ge(S["u_ps"], n + 1)
                dve.scalar_tensor_tensor(out=ab[q][:], in0=bU[:], scalar=1.0 / WS, in1=sg[q][:], op0=ALU.mult,
                                         op1=ALU.mult).then_inc(S["a_done"], 1)

            def act_lo(i, f):
                dve.wait_ge(S["ah_done"], NP * i + f + 1)
                dve.tensor_tensor(al[f][:], ab[f % 2][:], ah[f][:], ALU.subtract).then_inc(S["al_done"], 1)

            def shared_out(i):
                dve.wait_ge(S["d_ps"], NP * (i + 1))
                xi = xs[:, bass.ds(TB * i, TB), :]
                dve.scalar_tensor_tensor(out=xi, in0=bD[:].rearrange("p (t d) -> p t d", t=TB), scalar=1.0 / WS,
                                         in1=xi, op0=ALU.mult, op1=ALU.add).then_inc(S["x2_done"], 1)

            def logits(i):
                dve.wait_ge(S["r_ps"], i + 1)
                dve.tensor_scalar(logit[:], bR[:, 0:TB * E].rearrange("p (t e) -> p t e", e=E), 1.0 / WS, None,
                                  ALU.mult).then_inc(S["logit_done"], 1)
                dve.wait_ge(S["logit_done"], i + 1)
                if not isinstance(i, int) or i >= 1:
                    dve.wait_ge(S["best_done"], 2 * i)
                dve.nop(nofuse=True)
                for t in range(TB):
                    dve.max(top[:, t, :], logit[:, t, :]).then_inc(S["top_done"], 1)
                dve.wait_ge(S["top_done"], TB * (i + 1))
                dve.nop(nofuse=True)
                for t in range(TB):
                    dve.max_index(topi[:, t, :], top[:, t, :], logit[:, t, :]).then_inc(S["topi_done"], 1)
                dve.wait_ge(S["topi_done"], TB * (i + 1))
                for dst, src in ((best, top), (ei, topi)):
                    dve.tensor_copy(dst[:, :, bass.ds(TB * i, TB)], src[:, :, 0:2].rearrange("p t k -> p k t")
                                    ).then_inc(S["best_done"], 1)

            def expert_lo(e, j):
                dve.wait_ge(S["ex_hi"], 3 * e + j + 1)
                (hi, src), (lo, _) = expert_part(e, j, 0), expert_part(e, j, 1)
                dve.scalar_tensor_tensor(out=lo, in0=src, scalar=WS, in1=hi, op0=ALU.mult, op1=ALU.subtract
                                         ).then_inc(S["ex_lo"], 1)

            def shared_lo(m):
                dve.wait_ge(S["sh_hi"], m + 1)
                dve.scalar_tensor_tensor(out=ws_l[:, m, :], in0=stage_sh[:, m * KC * FS:(m + 1) * KC * FS], scalar=WS,
                                         in1=ws_h[:, m, :], op0=ALU.mult, op1=ALU.subtract).then_inc(S["sh_lo"], 1)

            def step(i, sh, ahead, before=False):
                if before:
                    shared_out(i - 2)
                if ahead:
                    norm(0, i + 1)
                keys(i)
                queries(i)
                sums(i)
                context(i)
                if sh:
                    swiglu(NP * (i - 1), 0)
                    logits(i - 1)
                    act_lo(i - 1, 0)
                context_lo(i)
                if sh:
                    swiglu(NP * (i - 1) + 1, 1)
                if ahead:
                    norm_apply(0, i + 1)
                if sh:
                    act_lo(i - 1, 1)
                    expert_lo(i, 0)
                residual(i)
                norm(1, i)
                if sh:
                    expert_lo(i, 1)
                    swiglu(NP * (i - 1) + 2, 0)
                    if ahead:
                        split_lo(0, i + 1)
                    norm_apply(1, i)
                    act_lo(i - 1, 2)
                    swiglu(NP * (i - 1) + 3, 1)
                    act_lo(i - 1, 3)
                    split_lo(1, i)
                else:
                    shared_lo(0)
                    norm_apply(1, i)
                    split_lo(0, i + 1)
                    shared_lo(1)
                    split_lo(1, i)
                    shared_lo(2)
                    expert_lo(i, 0)
                    expert_lo(i, 1)
                expert_lo(i, 2)

            dve.memset(keep[:], 1.0).then_inc(S["const_dve"], 1)
            dve.wait_ge(S["const_dve"], 1)
            dve.memset(keep[:, :, 0:1], 0.0).then_inc(S["const_dve"], 1)
            dve.wait_ge(S["const_pool"], 6)
            dve.tensor_copy(iota_f[:], iota_i[:]).then_inc(S["const_dve"], 1)
            dve.tensor_copy(iota16[:], iota_i[:]).then_inc(S["const_dve"], 1)
            dve.tensor_copy(tok_f[:], tok_i[:]).then_inc(S["const_dve"], 1)
            dve.tensor_copy(full_f[:], full_i[:]).then_inc(S["const_dve"], 1)
            dve.wait_ge(S["x0_in"], 16)
            norm(0, 0)
            norm_apply(0, 0)
            for part, n in ((slice(0, KC * D), "att_k"), (slice(KC * D, AW), "att")):
                dve.wait_ge(S[f"{n}_hi"], 1)
                dve.scalar_tensor_tensor(out=wa_l[:, part], in0=stage_att[:, part], scalar=WS, in1=wa_h[:, part],
                                         op0=ALU.mult, op1=ALU.subtract).then_inc(S[f"{n}_lo"], 1)
                if n == "att_k":
                    split_lo(0, 0)
            dve.wait_ge(S["bias_in"], 32)
            dve.tensor_scalar(bias1[:], bias[:, 0:2, :], 1.0, None, ALU.add).then_inc(S["bias_done"], 1)
            dve.tensor_scalar(bias_v[:], bias[:, 2, :], WS, None, ALU.mult).then_inc(S["bias_done"], 1)
            dve.wait_ge(S["bias_done"], 2)
            dve.wait_ge(S["x1_in"], 16)
            dve.wait_ge(S["const_dve"], 6)
            step(0, False, True)
            dve.wait_ge(S["x_in"], 16)
            step(1, True, True)
            with dve.Fori(2, B - 1) as i:
                step(i, True, True, True)
            step(B - 1, True, False, True)
            shared_out(B - 2)
            logits(B - 1)
            dve.wait_ge(S["best_done"], 2 * B)

            n = [0]

            def then(ins):
                n[0] += 1
                ins.then_inc(S["rt"], 1)
                dve.wait_ge(S["rt"], n[0])

            dve.tensor_tensor(sc_d[:], best[:, 1, :], best[:, 0, :], ALU.subtract).then_inc(S["dscore"], 1)
            wide = lambda a: a.rearrange("p (t o) -> p t o", o=1).to_broadcast((P, NT, E))
            for k in range(2):
                then(dve.tensor_tensor(oh[k][:], iota_f[:, 0:E].rearrange("p (o e) -> p o e", o=1).to_broadcast((P, NT, E)),
                                       wide(ei[:, k, :]), ALU.is_equal))
            by_tile = lambda a: a.rearrange("p e t -> p t e")
            dve.tensor_tensor(by_tile(member[:]), oh[0][:], oh[1][:], ALU.add).then_inc(S["member_done"], 1)
            swiglu(NP * (B - 1), 0)
            act_lo(B - 1, 0)
            dve.wait_ge(S["escore"], 1)
            then(dve.tensor_scalar(sc_1[:], sc_e[:], 1.0, None, ALU.add))
            then(dve.reciprocal(score[:, 0, :], sc_1[:]))
            then(dve.tensor_tensor(score[:, 1, :], sc_e[:], score[:, 0, :], ALU.mult))
            flat = lambda a: a.rearrange("p a b -> p (a b)")
            then(dve.tensor_copy(sc16[:], score[:].rearrange("p a b -> p (a b)")))
            then(dve.tensor_copy(vals[:, 1, :], sc16[:]))
            then(dve.tensor_tensor(vals[:, 2, :], score[:].rearrange("p a b -> p (a b)"), vals[:, 1, :], ALU.subtract))
            for k in range(2):
                then(dve.tensor_copy(vals[:, 0, k * NT:(k + 1) * NT], tok_f[:]))
            dve.wait_ge(S["rank_ps"], 1)
            then(dve.tensor_copy(flat(total), bQ[:, P:2 * P]))
            then(dve.tensor_copy(flat(before), bQ[:, 0:P]))
            then(dve.tensor_tensor_scan(flat(run), ones16[:], flat(total), 0.0, ALU.mult, ALU.add))
            then(dve.tensor_reduce(count[:], total, AX.X, ALU.add))
            then(dve.tensor_tensor(cmp, count[:].rearrange("p (e o) -> p e o", o=1).to_broadcast((P, E, NT)),
                                   full_f[:].rearrange("p (o t) -> p o t", o=1).to_broadcast((P, E, NT)), ALU.is_gt))
            then(dve.tensor_reduce(nblk[:], cmp, AX.X, ALU.add))
            then(dve.tensor_tensor_scan(bend[:], ones16[:, 0:E], nblk[:], 0.0, ALU.mult, ALU.add))
            then(dve.tensor_tensor(r1[:], bend[:], nblk[:], ALU.subtract))
            then(dve.tensor_tensor(r2[:], run[:, :, NT - 1], count[:], ALU.subtract))
            then(dve.scalar_tensor_tensor(out=base[:], in0=r1[:], scalar=float(P), in1=r2[:], op0=ALU.mult, op1=ALU.subtract))
            swiglu(NP * (B - 1) + 1, 1)
            act_lo(B - 1, 1)
            then(dve.tensor_tensor(s1, run, total, ALU.subtract))
            then(dve.tensor_tensor(s2, s1, before, ALU.add))
            then(dve.tensor_tensor(s3, s2, base[:].rearrange("p (e o) -> p e o", o=1).to_broadcast((P, E, NT)), ALU.add))
            for k in range(2):
                then(dve.tensor_tensor(pick[k][:], oh[k][:], by_tile(s3), ALU.mult))
                then(dve.tensor_reduce(slot[:, k * NT:(k + 1) * NT], pick[k][:], AX.X, ALU.add))
            then(dve.tensor_copy(slot_i[:], slot[:]))
            then(dve.tensor_scalar(blk_i[:], slot_i[:], 7, None, ALU.arith_shift_right))
            then(dve.tensor_scalar(pos_i[:], slot_i[:], P - 1, None, ALU.bitwise_and))
            then(dve.tensor_copy(blk_f[:], blk_i[:]))
            then(dve.tensor_copy(pos_f[:], pos_i[:]))
            then(dve.tensor_tensor(at_blk[:], iota_f[:, 0:NBP].rearrange("p (o b) -> p o b", o=1).to_broadcast((P, 2 * NT, NBP)),
                                   blk_f[:].rearrange("p (n o) -> p n o", o=1).to_broadcast((P, 2 * NT, NBP)), ALU.is_equal))
            for j in range(3):
                then(dve.tensor_tensor(put[:, :, j, :], at_blk[:],
                                       vals[:, j, :].rearrange("p (n o) -> p n o", o=1).to_broadcast((P, 2 * NT, NBP)), ALU.mult))
            swiglu(NP * (B - 1) + 2, 0)
            act_lo(B - 1, 2)
            for m in range(2 * NT):
                ins = dve.tensor_scalar(at_pos[:, m, :], iota16[:], pos_f[:, m:m + 1], None, ALU.is_equal)
            ins.then_inc(S["put_done"], 1)
            swiglu(NP * (B - 1) + 3, 1)
            act_lo(B - 1, 3)
            then(dve.tensor_tensor(bcmp[:], iota_f[:, 0:NBP].rearrange("p (b o) -> p b o", o=1).to_broadcast((P, NBP, E)),
                                   bend[:].rearrange("p (o e) -> p o e", o=1).to_broadcast((P, NBP, E)), ALU.is_ge))
            then(dve.tensor_reduce(bexp[:], bcmp[:], AX.X, ALU.add))
            then(dve.tensor_scalar(bexp_c[:], bexp[:], float(E - 1), None, ALU.min))
            dve.tensor_copy(blk_expert[:], bexp_c[:]).then_inc(S["bexp_done"], 1)
            shared_out(B - 1)
            dve.wait_ge(S["put_ps"], 1)
            then(dve.tensor_scalar(src_f[:], bV[:, 0:NBP], -1.0, 0.0, ALU.add, ALU.max))
            dve.tensor_copy(src_row[:], src_f[:]).then_inc(S["plan_done"], 1)
            then(dve.tensor_scalar(pad_f[:], bV[:, 0:NBP], 0.0, float(BIG), ALU.is_equal, ALU.mult))
            then(dve.scalar_tensor_tensor(out=dst_f[:], in0=bV[:, 0:NBP], scalar=-1.0, in1=pad_f[:], op0=ALU.add, op1=ALU.add))
            dve.tensor_copy(dst_row[:], dst_f[:]).then_inc(S["plan_done"], 1)
            then(dve.tensor_scalar(slot_lo[:], bV[:, 2 * NBP:3 * NBP], 1.0 / WS, None, ALU.mult))
            dve.scalar_tensor_tensor(out=slot_score[:], in0=bV[:, NBP:2 * NBP], scalar=1.0 / WS, in1=slot_lo[:],
                                     op0=ALU.mult, op1=ALU.add).then_inc(S["plan_done"], 1)
            dve.wait_ge(S["plan_done"], 3)

            def gather_lo(b, q):
                dve.wait_ge(S["gh_done"], b + 1)
                dve.tensor_tensor(gT_l[q].rearrange("p k l -> p (k l)"), bT[:, 0:KC * P],
                                  gT_h[q].rearrange("p k l -> p (k l)"), ALU.subtract).then_inc(S["gl_done"], 1)

            def routed_act_lo(b, q):
                dve.wait_ge(S["ah_done"], NP * B + b + 1)
                dve.tensor_tensor(al[q][:], bK[:], ah[q][:], ALU.subtract).then_inc(S["al_done"], 1)

            def result(b, q):
                dve.wait_ge(S["yl_done"], b + 1)
                if not isinstance(b, int) or b >= 2:
                    dve.wait_ge(S["scattered"], 16 * (b - 1))
                dve.scalar_tensor_tensor(out=ya[q], in0=(bV, bQ)[q][:, 0:D], scalar=slot_score[:, bass.ds(b, 1)],
                                         in1=yl[q], op0=ALU.mult, op1=ALU.add).then_inc(S["y_done"], 1)

            def routed(b, q, first, last):
                if not first:
                    routed_act_lo(b - 1, 1 - q)
                if not last:
                    gather_lo(b + 1, 1 - q)
                swiglu(NP * B + b, q)
                if not first:
                    result(b - 1, 1 - q)

            gather_lo(0, 0)
            routed(0, 0, True, False)
            routed(1, 1, False, False)
            routed(2, 0, False, False)
            with dve.Fori(3, NBLK - 2, 2) as b:
                routed(b, 1, False, False)
                routed(b + 1, 0, False, False)
            routed(NBLK - 2, 1, False, False)
            routed(NBLK - 1, 0, False, True)
            routed_act_lo(NBLK - 1, 0)
            result(NBLK - 1, 0)


def kernel(**inputs):
    import numpy as np
    import concourse.bacc as bacc
    from concourse.bass_utils import run_bass_kernel_spmd

    a = {k: np.asarray(v) for k, v in inputs.items()}

    def rows(w):
        return w.reshape(-1, P, w.shape[-1]).transpose(1, 0, 2).reshape(P, -1)

    att = [rows(a[f"L0_attn_W{m}"].T) for m in "kqvo"] + [rows(a["L0_ffn_router_w"])]
    w1, w2 = a["L0_ffn_w1"], a["L0_ffn_w2"]
    arrays = {
        "x": a["L0_attn_x"],
        "w_att": np.concatenate(att, axis=1),
        "w_bias": np.stack([a[f"L0_attn_b{m}"].reshape(-1, P).T for m in "qkv"], axis=1),
        "w_bo": a["L0_attn_bo"].reshape(1, -1),
        "w_shared": np.stack([rows(a[f"L0_ffn_w_{m}"]) for m in ("gate", "up", "down")], axis=1),
        "w_expert": np.stack([np.concatenate([rows(w1[e]), rows(w2[e])], axis=1) for e in range(w1.shape[0])]),
    }
    arrays = {f"in_{k}": np.ascontiguousarray(v) for k, v in arrays.items()}
    nc = bacc.Bacc("TRN2", target_bir_lowering=False, num_devices=1)
    args = [nc.dram_tensor(k, v.shape, mybir.dt.from_np(v.dtype), kind="ExternalInput").ap() for k, v in arrays.items()]
    out = nc.dram_tensor("out_y", a["L0_attn_x"].shape, F32, kind="ExternalOutput").ap()
    layer_kernel(nc, *args, out)
    r = run_bass_kernel_spmd(nc, [arrays], core_ids=[0])
    return r.results[0]["out_y"]
```

```python
from contextlib import ExitStack

import concourse.bass as bass
from concourse import mybir

ALU = mybir.AluOpType
ACT = mybir.ActivationFunctionType
AX = mybir.AxisListType
F32 = mybir.dt.float32
F16 = mybir.dt.float16
I32 = mybir.dt.int32
U32 = mybir.dt.uint32

P = 128
WS = 64.0
CS = 1.0 / 16.0
EPS = 1e-5


def layer_kernel(nc, x, w_att, w_bias, w_bo, w_shared, w_expert, out):
    B, L, D = x.shape
    NT = B * L // P
    TB = L // P
    KC = D // P
    HEAD_DIM = 16
    SCALE = float(HEAD_DIM) ** -0.5
    E = w_expert.shape[0]
    FS = w_shared.shape[2] // KC
    NP = FS // (2 * P)
    FE = w_expert.shape[2] // (2 * KC + D // P)
    FC = FE // P
    W1 = KC * 2 * FE
    NBLK = (2 * NT * P + E * (P - 1)) // P
    NBP = NBLK + 1
    BIG = 2 * NT * P
    POOL_TILES = 4
    AW = w_att.shape[1]

    scratch = nc.dram_tensor("xn2_rows", (NT * P, D), F32, kind="Internal").ap()
    xv = x.rearrange("b (t p) d -> b p t d", p=P)
    out_rows = out.rearrange("b l d -> (b l) d")
    outv = out.rearrange("b (t p) d -> b p t d", p=P)
    scr_v = scratch.rearrange("(b t p) d -> b p t d", p=P, t=TB)

    with ExitStack() as ctx:
        def sb(name, shape, dt=F32):
            return ctx.enter_context(nc.sbuf_tensor(name, shape, dt))

        def bank(name):
            return ctx.enter_context(nc.psum_tensor(name, [P, 512], F32))

        def sem(name):
            return ctx.enter_context(nc.semaphore(name))

        wa_h, wa_l = sb("wa_h", [P, AW], F16), sb("wa_l", [P, AW], F16)
        ws_h, ws_l = sb("ws_h", [P, 3, KC * FS], F16), sb("ws_l", [P, 3, KC * FS], F16)
        EW = w_expert.shape[2]
        we = sb("we", [P, 2, E, W1], F16)
        wd = sb("wd", [P, E, FC, 2, D], F16)
        stage = sb("stage", [P, EW])
        stage_att = wd[:, E // 2:E, :, :, :].rearrange("p e c s n -> p (e c s n)").bitcast(F32)[:, 0:AW]
        stage_sh = we[:, 1, 2:E, :].rearrange("p e n -> p (e n)").bitcast(F32)[:, 0:3 * KC * FS]

        def att_w(w, m):
            return w[:, m * KC * D:(m + 1) * KC * D].rearrange("p (k n) -> p k n", k=KC)

        def router_w(w):
            return w[:, 4 * KC * D:4 * KC * D + KC * E].rearrange("p (k n) -> p k n", k=KC)

        ident = sb("ident", [P, P])
        tri = sb("tri", [P, P], F16)
        ones16 = sb("ones16", [P, P], F16)
        keep = sb("keep", [P, 2, L], F16)
        minus_half = sb("minus_half", [P, TB])
        iota_i = sb("iota_i", [P, P], I32)
        iota_f = sb("iota_f", [P, P])
        iota16 = sb("iota16", [P, P], F16)
        tok_i = sb("tok_i", [P, NT], I32)
        tok_f = sb("tok_f", [P, NT])
        full_i = sb("full_i", [P, NT], I32)
        full_f = sb("full_f", [P, NT])

        xs = sb("xs", [P, NT, D])
        bias = sb("bias", [P, 3, KC])
        bias1 = sb("bias1", [P, 2, KC])
        bias_v = sb("bias_v", [P, KC])
        bo = sb("bo", [P, D])
        st = [sb(f"st{n}", [P, TB, 6]) for n in range(2)]
        mv = [sb(f"mv{n}", [P, TB, 2]) for n in range(2)]
        ve = [sb(f"ve{n}", [P, TB]) for n in range(2)]
        y0 = [sb(f"y0{n}", [P, TB]) for n in range(2)]
        nt_ = [sb(f"nt{n}", [P, TB]) for n in range(2)]
        nu = [sb(f"nu{n}", [P, TB]) for n in range(2)]
        rstd = [sb(f"rstd{n}", [P, TB]) for n in range(2)]
        xn = [sb(f"xn{n}", [P, TB, D]) for n in range(2)]
        xT_h = [sb(f"xTh{n}", [P, KC, L], F16) for n in range(2)]
        xT_l = [sb(f"xTl{n}", [P, KC, L], F16) for n in range(2)]
        work = sb("work", [P, 5, KC, L])
        ek, rk, eq, rq, kvs = (work[:, n, :, :] for n in range(5))
        phik, kv, phiq, cx = ek, rk, eq, rq
        cx_h, cx_l = sb("cx_h", [P, KC, L], F16), sb("cx_l", [P, KC, L], F16)
        sg = [sb(f"sg{n}", [P, 512]) for n in range(2)]
        ab = [sb(f"ab{n}", [P, 512]) for n in range(2)]
        ah = [sb(f"ah{n}", [P, 512], F16) for n in range(NP)]
        al = [sb(f"al{n}", [P, 512], F16) for n in range(NP)]

        bT, bK, bV, bQ, bG, bU, bD, bR = (bank(n) for n in ("bT", "bK", "bV", "bQ", "bG", "bU", "bD", "bR"))

        logit = sb("logit", [P, TB, E])
        top = sb("top", [P, TB, 8])
        topi = sb("topi", [P, TB, 8], U32)
        best = sb("best", [P, 2, NT])
        ei = sb("ei", [P, 2, NT])
        sc_d, sc_e, sc_1 = sb("sc_d", [P, NT]), sb("sc_e", [P, NT]), sb("sc_1", [P, NT])
        score = sb("score", [P, 2, NT])
        oh = sb("oh", [P, 2, NT, E])
        member = sb("member", [P, E, NT], F16)
        by_expert = lambda a: a.rearrange("p (e t) -> p e t", e=E)
        run, cmp = (by_expert(xn[0][:, 0, n * P:(n + 1) * P]) for n in range(2))
        before, total = (by_expert(bQ[:, n * P:(n + 1) * P]) for n in range(2))
        s1, s2 = (by_expert(xT_h[0][:, n, :].bitcast(F32)) for n in range(2))
        s3 = by_expert(xT_l[0][:, 0, :].bitcast(F32))
        count, nblk, bend = sb("count", [P, E]), sb("nblk", [P, E]), sb("bend", [P, E])
        r1, r2, base = sb("r1", [P, E]), sb("r2", [P, E]), sb("base", [P, E])
        pick = sb("pick", [P, 2, NT, E])
        slot = sb("slot", [P, 2 * NT])
        slot_i, blk_i, pos_i = (sb(n, [P, 2 * NT], I32) for n in ("slot_i", "blk_i", "pos_i"))
        blk16, pos_f = sb("blk16", [P, 2 * NT], F16), sb("pos_f", [P, 2 * NT])
        vals = sb("vals", [P, 3, 2 * NT], F16)
        at_pos = [w[:, n * P:(n + 1) * P] for w in (wa_h, wa_l) for n in range(NT)]
        work16 = work[:].rearrange("p a k l -> p (a k l)").bitcast(F16)
        put = work16[:, 0:6 * NT * NBP].rearrange("p (a n) -> p a n", n=2 * NT)
        at_blk = work16[:, 6 * NT * NBP:8 * NT * NBP].rearrange("p (b n) -> p b n", n=2 * NT)
        iota_blk = sb("iota_blk", [P, NBP, 2 * NT], F16)
        bcmp = sb("bcmp", [P, NBP, E])
        bexp, bexp_c = sb("bexp", [P, NBP]), sb("bexp_c", [P, NBP])
        blk_expert = sb("blk_expert", [P, NBP], I32)
        src_f, pad_f, dst_f = sb("src_f", [P, NBP]), sb("pad_f", [P, NBP]), sb("dst_f", [P, NBP])
        src_row, dst_row = sb("src_row", [P, NBP], U32), sb("dst_row", [P, NBP], U32)
        slot_lo, slot_score = sb("slot_lo", [P, NBP]), sb("slot_score", [P, NBP])

        gi = [sb(f"gi{n}", [P, 1], U32) for n in range(2)]
        si = [sb(f"si{n}", [P, 1], U32) for n in range(2)]
        xg = [work[:, n, :, :].rearrange("p k l -> p (k l)")[:, 0:D] for n in range(2)]
        gT_h = [cx_h[:, n, :].rearrange("p (k l) -> p k l", k=KC) for n in range(2)]
        gT_l = [cx_l[:, n, :].rearrange("p (k l) -> p k l", k=KC) for n in range(2)]
        ya = [xn[1][:, n, :] for n in range(2)]
        yl = [xn[0][:, n, :] for n in range(2)]

        names = """x0_in x1_in x_in att_k_in att_k_hi att_k_lo att_in bias_in up_in gate_in down_in ex_in att_hi att_lo sh_hi sh_scaled sh_lo sh_pool_lo ex_hi ex_lo
            const_pool const_dve bias_done xn2_saved out_saved
            ln1_step ln2_step ve1 ve2 pow1 pow2 xn1 xn2 xbo
            t1 t1_hi t1_lo t2 t2_hi t2_lo k_ps v_ps q_ps ek_done rk_done eq_done rq_done
            phik_done kv_done kvs_done phiq_done cx_done cxh_done cxl_done wo_ps x1_done
            g_ps u_ps sg_done a_done ah_done al_done d_ps x2_done
            r_ps logit_done top_done topi_done best_done
            rt u_copied iota_blk_done pos_done pool_pos_done dscore escore member_done rank_ps put_done put_ps plan_done bexp_done
            gi_done gathered0 gathered1 tx_ps gh_done gl_done ta_ps o_ps yl_done y_done si_done scattered""".split()
        S = {n: sem(n) for n in names}

        block = ctx.enter_context(nc.Block())

        def product(pe, dst, lhs_h, lhs_l, rhs_h, rhs_l, n, first=True, last=True, lone=False):
            steps = [(lhs_h, rhs_h), (lhs_h, rhs_l), (lhs_l, rhs_h)]
            for s, (a, b) in enumerate(steps):
                for c in range(n):
                    ins = pe.matmul(dst, a(c), b(c), start=first and s == 0 and c == 0,
                                    stop=last and s == 2 and c == n - 1, skip_group_check=lone)
            return ins

        def expert_part(e, j, lo):
            if j < 2:
                half = slice(j * W1 // 2, (j + 1) * W1 // 2)
                return we[:, lo, bass.ds(e, 1), half].rearrange("p o n -> p (o n)"), stage[:, half]
            return (wd[:, bass.ds(e, 1), :, lo, :].rearrange("p o c n -> p (o c) n"),
                    stage[:, W1:EW].rearrange("p (c n) -> p c n", n=D))

        SHARED = [(1, 1), (0, 0), (0, 1), (1, 0), (2, 0)]

        def shared_part(m, h, w):
            half = KC * FS // 2
            part = slice(h * half, (h + 1) * half) if m < 2 else slice(0, 2 * half)
            return w[:, m, part], stage_sh[:, m * 2 * half:(m + 1) * 2 * half][:, part]

        @block.sync
        def _(sp):
            sp.dma_start(xs[:, 0:TB, :], xv[0]).then_inc(S["x0_in"], 16)
            sp.dma_start(stage_att[:, 0:KC * D], w_att[:, 0:KC * D]).then_inc(S["att_k_in"], 16)
            sp.dma_start(stage_att[:, KC * D:AW], w_att[:, KC * D:AW]).then_inc(S["att_in"], 16)
            sp.dma_start(bias[:], w_bias).then_inc(S["bias_in"], 16)
            sp.dma_start(bo[:], w_bo.to_broadcast((P, D))).then_inc(S["bias_in"], 16)
            sp.dma_start(xs[:, TB:2 * TB, :], xv[1]).then_inc(S["x1_in"], 16)
            for m, part_in in ((1, "up_in"), (0, "gate_in"), (2, "down_in")):
                sp.dma_start(stage_sh[:, m * KC * FS:(m + 1) * KC * FS], w_shared[:, m, :]).then_inc(S[part_in], 16)
            sp.dma_start(xs[:, 2 * TB:NT, :].rearrange("p (b t) d -> p b t d", t=TB),
                         x[2:B].rearrange("b (t p) d -> p b t d", p=P)).then_inc(S["x_in"], 16)
            sp.dma_start(stage[:], w_expert[0]).then_inc(S["ex_in"], 16)

            def step(i, first=False):
                sp.wait_ge(S["xn2"], TB * (i + 1))
                sp.dma_start(scr_v[i] if isinstance(i, int) else scr_v[bass.ds(i, 1)].rearrange("o p t d -> (o p) t d"),
                             xn[1][:]).then_inc(S["xn2_saved"], 16)
                if not first:
                    sp.wait_ge(S["ex_hi"], 3 * i)
                    sp.wait_ge(S["ex_lo"], 3 * i)
                    src = w_expert[i] if isinstance(i, int) else w_expert[bass.ds(i, 1)].rearrange("o p n -> (o p) n")
                    sp.dma_start(stage[:], src).then_inc(S["ex_in"], 16)

            def save(i):
                sp.wait_ge(S["x2_done"], i + 1)
                dst = outv[i] if isinstance(i, int) else outv[bass.ds(i, 1)].rearrange("o p t d -> (o p) t d")
                sp.dma_start(dst, xs[:, bass.ds(TB * i, TB), :]).then_inc(S["out_saved"], 16)

            step(0, first=True)
            step(1)
            with sp.Fori(2, B - 1) as i:
                save(i - 2)
                step(i)
            save(B - 3)
            step(B - 1)
            save(B - 2)
            save(B - 1)
            sp.wait_ge(S["out_saved"], 16 * B)
            sp.wait_ge(S["scattered"], 16 * NBLK)

        @block.gpsimd
        def _(pool):
            pool.memset(ident[:], 0.0).then_inc(S["const_pool"], 1)
            pool.memset(ones16[:], 1.0).then_inc(S["const_pool"], 1)
            pool.memset(minus_half[:], -0.5).then_inc(S["const_pool"], 1)
            pool.iota(iota_i[:], pattern=[[1, P]], base=0, channel_multiplier=0).then_inc(S["const_pool"], 1)
            pool.iota(tok_i[:], pattern=[[P, NT]], base=1, channel_multiplier=1).then_inc(S["const_pool"], 1)
            pool.iota(full_i[:], pattern=[[P, NT]], base=0, channel_multiplier=0).then_inc(S["const_pool"], 1)
            pool.wait_ge(S["const_pool"], 6)
            pool.affine_select(out=ident[:], in_=ident[:], compare_op=ALU.not_equal, fill=1.0, base=0,
                               pattern=[[-1, P]], channel_multiplier=1).then_inc(S["const_pool"], 1)
            pool.affine_select(out=tri[:], in_=ones16[:], compare_op=ALU.is_ge, fill=0.0, base=-1,
                               pattern=[[1, P]], channel_multiplier=-1).then_inc(S["const_pool"], 1)

            def rsqrt(n, i):
                pool.wait_ge(S[f"ve{n + 1}"], i + 1)
                pool.tensor_tensor(y0[n][:], ve[n][:], minus_half[:], ALU.pow).then_inc(S[f"pow{n + 1}"], 1)

            def add_bo(i):
                pool.wait_ge(S["xn1"], TB * (i + 1))
                xi = xs[:, bass.ds(TB * i, TB), :]
                pool.tensor_tensor(xi, xi, bo[:].rearrange("p (o d) -> p o d", o=1).to_broadcast((P, TB, D)),
                                   ALU.add).then_inc(S["xbo"], 1)

            rsqrt(0, 0)
            pool.wait_ge(S["bias_in"], 32)
            add_bo(0)
            def shared_lo(n, m, h):
                (hi, src), (lo, _) = shared_part(m, h, ws_h), shared_part(m, h, ws_l)
                pool.wait_ge(S["sh_scaled"], n)
                pool.tensor_tensor(lo, src, hi, ALU.subtract).then_inc(S["sh_pool_lo"], 1)

            rsqrt(0, 1)
            shared_lo(1, 1, 1)
            add_bo(1)
            rsqrt(1, 0)
            shared_lo(2, 2, 0)
            with pool.Fori(1, B - 1) as i:
                rsqrt(0, i + 1)
                add_bo(i + 1)
                rsqrt(1, i)
            rsqrt(1, B - 1)
            pool.tensor_copy(iota_blk[:], iota_i[:, 0:NBP].rearrange("p (b o) -> p b o", o=1).to_broadcast((P, NBP, 2 * NT))
                             ).then_inc(S["iota_blk_done"], 1)
            for f in range(NP):
                pool.wait_ge(S["sg_done"], NP * (B - 1) + f + 1)
                pool.wait_ge(S["u_copied"], f + 1)
                pool.tensor_tensor(ab[f % 2][:], ab[f % 2][:], sg[f % 2][:], ALU.mult).then_inc(S["a_done"], 1)
                if f < NP - 1:
                    pool.wait_ge(S["ah_done"], NP * (B - 1) + f + 1)
                    pool.tensor_tensor(al[f][:], ab[f % 2][:], ah[f][:], ALU.subtract).then_inc(S["al_done"], 1)
                if f == 1:
                    pool.wait_ge(S["pos_done"], 1)
                    for m in range(POOL_TILES):
                        pool.tensor_scalar(at_pos[m], iota16[:], pos_f[:, m:m + 1], None, ALU.is_equal
                                           ).then_inc(S["pool_pos_done"], 1)

            pool.wait_ge(S["plan_done"], 1)
            pool.wait_ge(S["xn2_saved"], 16 * B)

            def gather(b, q, fresh):
                if not fresh:
                    pool.wait_ge(S["tx_ps"], b - 1)
                pool.tensor_copy(gi[q][:], src_row[:, bass.ds(b, 1)]).then_inc(S["gi_done"], 1)
                pool.wait_ge(S["gi_done"], b + 1)
                pool.nop(nofuse=True)
                pool.indirect_dma_start(xg[q], None, scratch, bass.IndirectOffsetOnAxis(ap=gi[q][:], axis=0)
                                        ).then_inc(S[f"gathered{q}"], 16)

            def scatter(b, q):
                if not isinstance(b, int) or b >= 1:
                    pool.wait_ge(S["scattered"], 16 * b)
                pool.tensor_copy(si[q][:], dst_row[:, bass.ds(b, 1)]).then_inc(S["si_done"], 1)
                pool.wait_ge(S["si_done"], b + 1)
                pool.wait_ge(S["y_done"], b + 1)
                pool.nop(nofuse=True)
                pool.indirect_dma_start(out_rows, bass.IndirectOffsetOnAxis(ap=si[q][:], axis=0), ya[q], None,
                                        bounds_check=NT * P - 1, oob_is_err=False, compute_op=ALU.add
                                        ).then_inc(S["scattered"], 16)

            for b in range(4):
                gather(b, b % 2, b < 2)
            pool.wait_ge(S["out_saved"], 16 * B)
            gather(4, 0, False)
            scatter(0, 0)
            with pool.Fori(1, NBLK - 4, 2) as b:
                for q in range(2):
                    gather(b + 4 + q, 1 - q, False)
                    scatter(b + q, 1 - q)
            for b in range(NBLK - 4, NBLK):
                scatter(b, b % 2)

        @block.tensor
        def _(pe):
            def norm_T(n, i):
                pe.wait_ge(S[f"xn{n + 1}"], TB * (i + 1))
                if n == 0:
                    if not isinstance(i, int) or i >= 2:
                        pe.wait_ge(S["t2_lo"], i - 1)
                    if not isinstance(i, int) or i >= 1:
                        pe.wait_ge(S["t1_lo"], i)
                else:
                    pe.wait_ge(S["t1_lo"], i + 1 if isinstance(i, int) and i == B - 1 else i + 2)
                for t in range(TB):
                    for k in range(KC):
                        ins = pe.transpose(bT[:, k * L + t * P:k * L + (t + 1) * P],
                                           xn[n][:, t, k * P:(k + 1) * P], ident[:])
                ins.then_inc(S[f"t{n + 1}"], 1)

            def project(i):
                pe.wait_ge(S["t1_lo"], i + 1)
                for m, dst, done in ((0, bK, "k_ps"), (1, bQ, "q_ps"), (2, bV, "v_ps")):
                    if isinstance(i, int) and i == 1 and m == 1:
                        norm_T(1, 0)
                    if not isinstance(i, int) or i >= 1:
                        if m == 0:
                            pe.wait_ge(S["x1_done"], i)
                        elif m == 1:
                            pe.wait_ge(S["rq_done"], KC * i)
                        else:
                            pe.wait_ge(S["kv_done"], KC * i)
                    elif m == 1:
                        pe.wait_ge(S["att_lo"], 1)
                    wh, wl = att_w(wa_h, m), att_w(wa_l, m)
                    for c in range(KC):
                        ins = product(pe, dst[:, c * L:(c + 1) * L],
                                      lambda k: wh[:, k, c * P:(c + 1) * P], lambda k: wl[:, k, c * P:(c + 1) * P],
                                      lambda k: xT_h[0][:, k, :], lambda k: xT_l[0][:, k, :], KC)
                    ins.then_inc(S[done], 1)

            def attend_out(i):
                pe.wait_ge(S["cxl_done"], i + 1)
                wh, wl = att_w(wa_h, 3), att_w(wa_l, 3)
                for t in range(TB):
                    ins = product(pe, bK[:, t * D:(t + 1) * D],
                                  lambda k: cx_h[:, k, t * P:(t + 1) * P], lambda k: cx_l[:, k, t * P:(t + 1) * P],
                                  lambda k: wh[:, k, :], lambda k: wl[:, k, :], KC)
                ins.then_inc(S["wo_ps"], 1)

            def route(i):
                pe.wait_ge(S["t2_lo"], i + 1)
                if not isinstance(i, int) or i >= 1:
                    pe.wait_ge(S["logit_done"], i)
                wh, wl = router_w(wa_h), router_w(wa_l)
                for t in range(TB):
                    ins = product(pe, bR[:, t * E:(t + 1) * E],
                                  lambda k: xT_h[1][:, k, t * P:(t + 1) * P], lambda k: xT_l[1][:, k, t * P:(t + 1) * P],
                                  lambda k: wh[:, k, :], lambda k: wl[:, k, :], KC)
                ins.then_inc(S["r_ps"], 1)

            def gate_up(i, f):
                n = NP * i + f
                for m, dst, done, free in ((0, bG, "g_ps", "sg_done"), (1, bU, "u_ps", "a_done")):
                    if not isinstance(i, int) or n >= 1:
                        pe.wait_ge(S[free], n)
                    wh = ws_h[:, m, :].rearrange("p (k n) -> p k n", k=KC)
                    wl = ws_l[:, m, :].rearrange("p (k n) -> p k n", k=KC)
                    for c in range(2):
                        at = (2 * f + c) * P
                        ins = product(pe, dst[:, c * L:(c + 1) * L],
                                      lambda k: wh[:, k, at:at + P], lambda k: wl[:, k, at:at + P],
                                      lambda k: xT_h[1][:, k, :], lambda k: xT_l[1][:, k, :], KC)
                    ins.then_inc(S[done], 1)

            def down(i, f):
                pe.wait_ge(S["al_done"], NP * i + f + 1)
                if f == 0 and (not isinstance(i, int) or i >= 1):
                    pe.wait_ge(S["x2_done"], i)
                wh = ws_h[:, 2, :].rearrange("p (c n) -> p c n", n=D)
                wl = ws_l[:, 2, :].rearrange("p (c n) -> p c n", n=D)
                for t in range(TB):
                    ins = product(pe, bD[:, t * D:(t + 1) * D],
                                  lambda c: ah[f][:, c * L + t * P:c * L + (t + 1) * P],
                                  lambda c: al[f][:, c * L + t * P:c * L + (t + 1) * P],
                                  lambda c: wh[:, 2 * f + c, :], lambda c: wl[:, 2 * f + c, :], 2,
                                  first=(f == 0 and t == 0), last=(f == NP - 1), lone=True)
                ins.then_inc(S["d_ps"], 1)

            def step(i, shared, ahead):
                project(i)
                if shared:
                    route(i - 1)
                    if isinstance(i, int) and i == 1:
                        pe.wait_ge(S["sh_lo"], 3)
                        pe.wait_ge(S["sh_pool_lo"], 1)
                    gate_up(i - 1, 0)
                    gate_up(i - 1, 1)
                    if isinstance(i, int) and i == 1:
                        pe.wait_ge(S["sh_pool_lo"], 2)
                    down(i - 1, 0)
                attend_out(i)
                if shared:
                    gate_up(i - 1, 2)
                if ahead:
                    norm_T(0, i + 1)
                if shared:
                    gate_up(i - 1, 3)
                    down(i - 1, 1)
                if shared:
                    norm_T(1, i)
                    down(i - 1, 2)
                    down(i - 1, 3)

            pe.wait_ge(S["const_pool"], 8)
            norm_T(0, 0)
            pe.wait_ge(S["att_k_lo"], 1)
            step(0, False, True)
            step(1, True, True)
            with pe.Fori(2, B - 1) as i:
                step(i, True, True)
            step(B - 1, True, False)
            route(B - 1)
            gate_up(B - 1, 0)
            pe.wait_ge(S["member_done"], 1)
            mem = member[:].rearrange("p e t -> p (e t)")
            pe.matmul(bQ[:, 0:P], tri[:], mem, start=True, stop=True)
            pe.matmul(bQ[:, P:2 * P], ones16[:], mem, start=True, stop=True).then_inc(S["rank_ps"], 1)
            gate_up(B - 1, 1)
            down(B - 1, 0)
            gate_up(B - 1, 2)
            down(B - 1, 1)
            gate_up(B - 1, 3)
            pe.wait_ge(S["put_done"], 1)
            pe.wait_ge(S["pool_pos_done"], POOL_TILES)
            for n in range(2 * NT):
                ins = pe.matmul(bV[:, 0:3 * NBP], at_pos[n], put[:, :, n], start=(n == 0), stop=(n == 2 * NT - 1))
            ins.then_inc(S["put_ps"], 1)
            down(B - 1, 2)

            def turn_x(b, q):
                pe.wait_ge(S[f"gathered{q}"], 8 * (b - q) + 16)
                for k in range(KC):
                    ins = pe.transpose(bT[:, k * P:(k + 1) * P], xg[q][:, k * P:(k + 1) * P], ident[:])
                ins.then_inc(S["tx_ps"], 1)

            def turn_a(b, q):
                pe.wait_ge(S["a_done"], NP * B + b + 1)
                for c in range(FC):
                    ins = pe.transpose(bK[:, c * P:(c + 1) * P], ab[q][:, c * P:(c + 1) * P], ident[:])
                ins.then_inc(S["ta_ps"], 1)

            def expert_up(b, q, e, half):
                dst, done = ((bG, "g_ps"), (bU, "u_ps"))[half]
                if half == 0:
                    pe.wait_ge(S["gl_done"], b + 1)
                w = [we[:, lo, bass.ds(e, 1), :].rearrange("p o (k h n) -> p (o k) h n", k=KC, h=2) for lo in range(2)]
                product(pe, dst[:], lambda k: gT_h[q][:, k, :], lambda k: gT_l[q][:, k, :],
                        lambda k: w[0][:, k, half, :], lambda k: w[1][:, k, half, :], KC).then_inc(S[done], 1)

            def expert_down(b, q, e):
                pe.wait_ge(S["al_done"], NP * B + b + 1)
                w = wd[:, bass.ds(e, 1), :, :, :].rearrange("p o c s n -> p (o c) (s n)")
                dst = (bV, bQ)[q]
                for c in range(FC):
                    pe.matmul(dst[:], ah[q][:, c * P:(c + 1) * P], w[:, c, :], start=(c == 0), stop=False,
                              skip_group_check=True)
                for c in range(FC):
                    ins = pe.matmul(dst[:, 0:D], al[q][:, c * P:(c + 1) * P], w[:, c, 0:D], start=False,
                                    stop=(c == FC - 1), skip_group_check=True)
                ins.then_inc(S["o_ps"], 1)

            expert_reg = [pe.alloc_register(f"expert_reg{q}") for q in range(2)]

            def load_expert(b, q):
                pe.reg_load(expert_reg[q], blk_expert[0:1, bass.ds(b, 1)])

            def expert(q):
                return pe.snap(expert_reg[q], min_val=0, max_val=E - 1)

            def routed(b, q, first, last):
                if not first:
                    turn_a(b - 1, 1 - q)
                e = expert(q)
                expert_up(b, q, e, 0)
                if not last:
                    turn_x(b + 1, 1 - q)
                expert_up(b, q, e, 1)
                if not first:
                    expert_down(b - 1, 1 - q, expert(1 - q))
                if not last:
                    load_expert(b + 1, 1 - q)

            pe.wait_ge(S["bexp_done"], 1)
            pe.wait_ge(S["x1_done"], B)
            load_expert(0, 0)
            turn_x(0, 0)
            down(B - 1, NP - 1)
            pe.wait_ge(S["ex_lo"], 3 * E)
            routed(0, 0, True, False)
            routed(1, 1, False, False)
            routed(2, 0, False, False)
            with pe.Fori(3, NBLK - 2, 2) as b:
                routed(b, 1, False, False)
                routed(b + 1, 0, False, False)
            routed(NBLK - 2, 1, False, False)
            routed(NBLK - 1, 0, False, True)
            turn_a(NBLK - 1, 0)
            expert_down(NBLK - 1, 0, expert(0))

        @block.scalar
        def _(act):
            def split_hi(n, i):
                act.wait_ge(S[f"t{n + 1}"], i + 1)
                if not isinstance(i, int) or i >= 1:
                    if n == 0:
                        act.wait_ge(S["v_ps"], i)
                    else:
                        act.wait_ge(S["r_ps"], i)
                        act.wait_ge(S["u_ps"], NP * i)
                act.activation(xT_h[n][:].rearrange("p k l -> p (k l)"), bT[:], ACT.Copy).then_inc(S[f"t{n + 1}_hi"], 1)

            def exps(i):
                for src, ready, e, r, m, ed, rd, used in ((bK, "k_ps", ek, rk, 1, "ek_done", "rk_done", "kvs_done"),
                                                          (bQ, "q_ps", eq, rq, 0, "eq_done", "rq_done", "cxl_done")):
                    act.wait_ge(S[ready], i + 1)
                    if not isinstance(i, int) or i >= 1:
                        act.wait_ge(S[used], i)
                    for c in range(KC):
                        act.activation(e[:, c, :], src[:, c * L:(c + 1) * L], ACT.Exp, bias=bias[:, m, c:c + 1],
                                       scale=1.0 / WS).then_inc(S[ed], 1)
                    for c in range(KC):
                        act.activation(r[:, c, :], src[:, c * L:(c + 1) * L], ACT.Identity, bias=bias1[:, m, c:c + 1],
                                       scale=1.0 / WS).then_inc(S[rd], 1)

            def context_hi(i):
                act.wait_ge(S["cx_done"], i + 1)
                if not isinstance(i, int) or i >= 1:
                    act.wait_ge(S["wo_ps"], i)
                act.activation(cx_h[:], cx, ACT.Copy).then_inc(S["cxh_done"], 1)

            def silu(n, q):
                act.wait_ge(S["g_ps"], n + 1)
                act.wait_ge(S["a_done"], n)
                act.activation(sg[q][:], bG[:], ACT.Silu, scale=1.0 / WS).then_inc(S["sg_done"], 1)

            def act_hi(i, f):
                n = NP * i + f
                act.wait_ge(S["a_done"], n + 1)
                if not isinstance(i, int) or i >= 1:
                    act.wait_ge(S["d_ps"], n - NP + 1)
                act.activation(ah[f][:], ab[f % 2][:], ACT.Copy).then_inc(S["ah_done"], 1)

            def expert_hi(e, j):
                if j == 0:
                    act.wait_ge(S["ex_in"], 16 * (e + 1))
                dst, src = expert_part(e, j, 0)
                act.activation(dst, src, ACT.Copy, scale=WS).then_inc(S["ex_hi"], 1)

            def shared_hi(m, h):
                dst, src = shared_part(m, h, ws_h)
                act.activation(dst, src, ACT.Copy, scale=WS).then_inc(S["sh_hi"], 1)

            def shared_scale(m, h):
                _, src = shared_part(m, h, ws_h)
                act.activation(src, src, ACT.Copy, scale=WS).then_inc(S["sh_scaled"], 1)

            def step(i, sh, ahead):
                exps(i)
                if sh:
                    silu(NP * (i - 1), 0)
                if not sh:
                    act.wait_ge(S["up_in"], 16)
                    shared_hi(1, 1)
                    shared_scale(1, 1)
                    act.wait_ge(S["gate_in"], 16)
                    shared_hi(0, 0)
                context_hi(i)
                if sh:
                    act_hi(i - 1, 0)
                    silu(NP * (i - 1) + 1, 1)
                else:
                    shared_hi(0, 1)
                    shared_hi(1, 0)
                    act.wait_ge(S["down_in"], 16)
                    shared_hi(2, 0)
                    split_hi(0, i + 1)
                    shared_scale(2, 0)
                    split_hi(1, i)
                    return
                expert_hi(i - 1, 0)
                act_hi(i - 1, 1)
                expert_hi(i - 1, 1)
                silu(NP * (i - 1) + 2, 0)
                if ahead:
                    split_hi(0, i + 1)
                act_hi(i - 1, 2)
                silu(NP * (i - 1) + 3, 1)
                expert_hi(i - 1, 2)
                act_hi(i - 1, 3)
                split_hi(1, i)

            act.wait_ge(S["att_k_in"], 16)
            act.activation(wa_h[:, 0:KC * D], stage_att[:, 0:KC * D], ACT.Copy, scale=WS).then_inc(S["att_k_hi"], 1)
            split_hi(0, 0)
            act.wait_ge(S["att_in"], 16)
            act.activation(wa_h[:, KC * D:AW], stage_att[:, KC * D:AW], ACT.Copy, scale=WS).then_inc(S["att_hi"], 1)
            act.wait_ge(S["bias_done"], 2)
            step(0, False, True)
            step(1, True, True)
            with act.Fori(2, B - 1) as i:
                step(i, True, True)
            step(B - 1, True, False)
            act.wait_ge(S["dscore"], 1)
            act.activation(sc_e[:], sc_d[:], ACT.Exp).then_inc(S["escore"], 1)
            for f in range(NP):
                silu(NP * (B - 1) + f, f % 2)
                if f == NP - 1:
                    expert_hi(E - 1, 0)
                act.wait_ge(S["u_ps"], NP * (B - 1) + f + 1)
                act.wait_ge(S["al_done"], NP * (B - 1) + f - 1)
                act.activation(ab[f % 2][:], bU[:], ACT.Copy, scale=1.0 / WS).then_inc(S["u_copied"], 1)
                act_hi(B - 1, f)
            for j in range(1, 3):
                expert_hi(E - 1, j)

            def gather_hi(b, q):
                act.wait_ge(S["tx_ps"], b + 1)
                if not isinstance(b, int) or b >= 2:
                    act.wait_ge(S["u_ps"], NP * B + b - 1)
                act.activation(gT_h[q].rearrange("p k l -> p (k l)"), bT[:, 0:KC * P], ACT.Copy).then_inc(S["gh_done"], 1)

            def routed_act_hi(b, q):
                act.wait_ge(S["ta_ps"], b + 1)
                if isinstance(b, int) and b < 2:
                    act.wait_ge(S["d_ps"], NP * B)
                else:
                    act.wait_ge(S["o_ps"], b - 1)
                act.activation(ah[q][:], bK[:], ACT.Copy).then_inc(S["ah_done"], 1)

            def result_lo(b, q):
                act.wait_ge(S["o_ps"], b + 1)
                if not isinstance(b, int) or b >= 2:
                    act.wait_ge(S["y_done"], b - 1)
                act.activation(yl[q], (bV, bQ)[q][:, D:2 * D], ACT.Copy, scale=slot_score[:, bass.ds(b, 1)]
                               ).then_inc(S["yl_done"], 1)

            def routed(b, q, first, last):
                if not first:
                    routed_act_hi(b - 1, 1 - q)
                silu(NP * B + b, q)
                if not last:
                    gather_hi(b + 1, 1 - q)
                if not first:
                    result_lo(b - 1, 1 - q)

            gather_hi(0, 0)
            routed(0, 0, True, False)
            routed(1, 1, False, False)
            routed(2, 0, False, False)
            with act.Fori(3, NBLK - 2, 2) as b:
                routed(b, 1, False, False)
                routed(b + 1, 0, False, False)
            routed(NBLK - 2, 1, False, False)
            routed(NBLK - 1, 0, False, True)
            routed_act_hi(NBLK - 1, 0)
            result_lo(NBLK - 1, 0)

        @block.vector
        def _(dve):
            LN = 7

            def norm(n, i):
                s = S[f"ln{n + 1}_step"]
                at = LN * i
                for t in range(TB):
                    dve.bn_stats(st[n][:, t, :], xs[:, bass.ds(TB * i + t, 1), :].rearrange("p o d -> p (o d)")).then_inc(s, 1)
                dve.wait_ge(s, at + 2)
                dve.nop(nofuse=True)
                for t in range(TB):
                    dve.bn_aggr(mv[n][:, t, :], st[n][:, t, :]).then_inc(s, 1)
                dve.wait_ge(s, at + 4)
                dve.tensor_scalar(ve[n][:], mv[n][:, :, 1], EPS, None, ALU.add).then_inc(S[f"ve{n + 1}"], 1)

            def newton(n, i, k):
                s = S[f"ln{n + 1}_step"]
                if k == 0:
                    dve.wait_ge(S[f"pow{n + 1}"], i + 1)
                    dve.tensor_tensor(nt_[n][:], y0[n][:], y0[n][:], ALU.mult).then_inc(s, 1)
                elif k == 1:
                    dve.wait_ge(s, LN * i + 5)
                    dve.scalar_tensor_tensor(out=nu[n][:], in0=nt_[n][:], scalar=-0.5, in1=ve[n][:], op0=ALU.mult,
                                             op1=ALU.mult).then_inc(s, 1)
                else:
                    dve.wait_ge(s, LN * i + 6)
                    dve.scalar_tensor_tensor(out=rstd[n][:], in0=nu[n][:], scalar=1.5, in1=y0[n][:], op0=ALU.add,
                                             op1=ALU.mult).then_inc(s, 1)

            def normed(n, i):
                dve.wait_ge(S[f"ln{n + 1}_step"], LN * (i + 1))
                if not isinstance(i, int) or i >= 1:
                    dve.wait_ge(S[f"t{n + 1}"], i)
                    if n == 1:
                        dve.wait_ge(S["xn2_saved"], 16 * i)
                for t in range(TB):
                    dve.tensor_scalar(xn[n][:, t, :], xs[:, bass.ds(TB * i + t, 1), :].rearrange("p o d -> p (o d)"),
                                      mv[n][:, t, 0:1], rstd[n][:, t:t + 1], ALU.subtract, ALU.mult
                                      ).then_inc(S[f"xn{n + 1}"], 1)

            def norm_apply(n, i):
                for k in range(3):
                    newton(n, i, k)
                normed(n, i)

            def split_lo(n, i):
                dve.wait_ge(S[f"t{n + 1}_hi"], i + 1)
                dve.tensor_tensor(xT_l[n][:].rearrange("p k l -> p (k l)"), bT[:],
                                  xT_h[n][:].rearrange("p k l -> p (k l)"), ALU.subtract).then_inc(S[f"t{n + 1}_lo"], 1)

            def keys(i):
                dve.wait_ge(S["ek_done"], KC * (i + 1))
                dve.wait_ge(S["rk_done"], KC * (i + 1))
                dve.scalar_tensor_tensor(out=phik, in0=ek, scalar=1.0, in1=rk, op0=ALU.min, op1=ALU.max
                                         ).then_inc(S["phik_done"], 1)
                dve.wait_ge(S["phik_done"], i + 1)
                dve.wait_ge(S["v_ps"], i + 1)
                for c in range(KC):
                    dve.scalar_tensor_tensor(out=kv[:, c, :], in0=bV[:, c * L:(c + 1) * L], scalar=bias_v[:, c:c + 1],
                                             in1=phik[:, c, :], op0=ALU.add, op1=ALU.mult).then_inc(S["kv_done"], 1)

            def sums(i):
                dve.wait_ge(S["kv_done"], KC * (i + 1))
                dve.tensor_tensor_scan(kvs.rearrange("p k l -> p (k l)"), keep[:].rearrange("p k l -> p (k l)"),
                                       kv.rearrange("p k l -> p (k l)"), 0.0, ALU.mult, ALU.add
                                       ).then_inc(S["kvs_done"], 1)

            def queries(i):
                dve.wait_ge(S["eq_done"], KC * (i + 1))
                dve.wait_ge(S["rq_done"], KC * (i + 1))
                dve.scalar_tensor_tensor(out=phiq, in0=eq, scalar=1.0, in1=rq, op0=ALU.min, op1=ALU.max
                                         ).then_inc(S["phiq_done"], 1)

            def context(i):
                dve.wait_ge(S["phiq_done"], i + 1)
                dve.wait_ge(S["kvs_done"], i + 1)
                if not isinstance(i, int) or i >= 1:
                    dve.wait_ge(S["cxh_done"], i)
                dve.scalar_tensor_tensor(out=cx, in0=kvs, scalar=SCALE * CS / WS, in1=phiq, op0=ALU.mult,
                                         op1=ALU.mult).then_inc(S["cx_done"], 1)

            def context_lo(i):
                dve.wait_ge(S["cxh_done"], i + 1)
                dve.tensor_tensor(cx_l[:], cx, cx_h[:], ALU.subtract).then_inc(S["cxl_done"], 1)

            def residual(i):
                dve.wait_ge(S["wo_ps"], i + 1)
                dve.wait_ge(S["xbo"], i + 1)
                xi = xs[:, bass.ds(TB * i, TB), :]
                dve.scalar_tensor_tensor(out=xi, in0=bK[:].rearrange("p (t d) -> p t d", t=TB), scalar=1.0 / (WS * CS),
                                         in1=xi, op0=ALU.mult, op1=ALU.add).then_inc(S["x1_done"], 1)
                dve.wait_ge(S["x1_done"], i + 1)
                dve.nop(nofuse=True)

            def swiglu(n, q):
                dve.wait_ge(S["sg_done"], n + 1)
                dve.wait_ge(S["u_ps"], n + 1)
                dve.scalar_tensor_tensor(out=ab[q][:], in0=bU[:], scalar=1.0 / WS, in1=sg[q][:], op0=ALU.mult,
                                         op1=ALU.mult).then_inc(S["a_done"], 1)

            def act_lo(i, f):
                dve.wait_ge(S["ah_done"], NP * i + f + 1)
                dve.tensor_tensor(al[f][:], ab[f % 2][:], ah[f][:], ALU.subtract).then_inc(S["al_done"], 1)

            def shared_out(i):
                dve.wait_ge(S["d_ps"], NP * (i + 1))
                xi = xs[:, bass.ds(TB * i, TB), :]
                dve.scalar_tensor_tensor(out=xi, in0=bD[:].rearrange("p (t d) -> p t d", t=TB), scalar=1.0 / WS,
                                         in1=xi, op0=ALU.mult, op1=ALU.add).then_inc(S["x2_done"], 1)

            def logits(i, k):
                if k == 0:
                    dve.wait_ge(S["r_ps"], i + 1)
                    dve.tensor_scalar(logit[:], bR[:, 0:TB * E].rearrange("p (t e) -> p t e", e=E), 1.0 / WS, None,
                                      ALU.mult).then_inc(S["logit_done"], 1)
                elif k == 1:
                    dve.wait_ge(S["logit_done"], i + 1)
                    dve.nop(nofuse=True)
                    for t in range(TB):
                        dve.max(top[:, t, :], logit[:, t, :]).then_inc(S["top_done"], 1)
                elif k == 2:
                    dve.wait_ge(S["top_done"], TB * (i + 1))
                    dve.nop(nofuse=True)
                    for t in range(TB):
                        dve.max_index(topi[:, t, :], top[:, t, :], logit[:, t, :]).then_inc(S["topi_done"], 1)
                else:
                    dve.wait_ge(S["topi_done"], TB * (i + 1))
                    for dst, src in ((best, top), (ei, topi)):
                        dve.tensor_copy(dst[:, :, bass.ds(TB * i, TB)], src[:, :, 0:2].rearrange("p t k -> p k t")
                                        ).then_inc(S["best_done"], 1)

            def expert_lo(e, j):
                dve.wait_ge(S["ex_hi"], 3 * e + j + 1)
                (hi, src), (lo, _) = expert_part(e, j, 0), expert_part(e, j, 1)
                dve.scalar_tensor_tensor(out=lo, in0=src, scalar=WS, in1=hi, op0=ALU.mult, op1=ALU.subtract
                                         ).then_inc(S["ex_lo"], 1)

            def shared_lo(m, h):
                dve.wait_ge(S["sh_hi"], SHARED.index((m, h)) + 1)
                (hi, src), (lo, _) = shared_part(m, h, ws_h), shared_part(m, h, ws_l)
                dve.scalar_tensor_tensor(out=lo, in0=src, scalar=WS, in1=hi, op0=ALU.mult, op1=ALU.subtract
                                         ).then_inc(S["sh_lo"], 1)

            def step(i, sh, ahead, before=False):
                if before:
                    shared_out(i - 2)
                if ahead:
                    norm(0, i + 1)
                keys(i)
                if ahead:
                    newton(0, i + 1, 0)
                queries(i)
                if ahead:
                    newton(0, i + 1, 1)
                sums(i)
                if ahead:
                    newton(0, i + 1, 2)
                context(i)
                if sh:
                    swiglu(NP * (i - 1), 0)
                    logits(i - 1, 0)
                context_lo(i)
                if sh:
                    logits(i - 1, 1)
                    act_lo(i - 1, 0)
                    logits(i - 1, 2)
                    swiglu(NP * (i - 1) + 1, 1)
                if not sh:
                    shared_lo(0, 0)
                if ahead:
                    normed(0, i + 1)
                if sh:
                    act_lo(i - 1, 1)
                    logits(i - 1, 3)
                residual(i)
                norm(1, i)
                if not sh:
                    split_lo(0, i + 1)
                    norm_apply(1, i)
                    shared_lo(0, 1)
                    shared_lo(1, 0)
                    split_lo(1, i)
                    return
                expert_lo(i - 1, 0)
                newton(1, i, 0)
                swiglu(NP * (i - 1) + 2, 0)
                newton(1, i, 1)
                if ahead:
                    split_lo(0, i + 1)
                newton(1, i, 2)
                act_lo(i - 1, 2)
                normed(1, i)
                swiglu(NP * (i - 1) + 3, 1)
                act_lo(i - 1, 3)
                split_lo(1, i)
                expert_lo(i - 1, 1)
                if ahead:
                    expert_lo(i - 1, 2)

            dve.memset(keep[:], 1.0).then_inc(S["const_dve"], 1)
            dve.wait_ge(S["const_dve"], 1)
            dve.memset(keep[:, :, 0:1], 0.0).then_inc(S["const_dve"], 1)
            dve.wait_ge(S["const_pool"], 6)
            dve.tensor_copy(iota_f[:], iota_i[:]).then_inc(S["const_dve"], 1)
            dve.tensor_copy(iota16[:], iota_i[:]).then_inc(S["const_dve"], 1)
            dve.tensor_copy(tok_f[:], tok_i[:]).then_inc(S["const_dve"], 1)
            dve.tensor_copy(full_f[:], full_i[:]).then_inc(S["const_dve"], 1)
            dve.wait_ge(S["x0_in"], 16)
            norm(0, 0)
            norm_apply(0, 0)
            for part, n in ((slice(0, KC * D), "att_k"), (slice(KC * D, AW), "att")):
                dve.wait_ge(S[f"{n}_hi"], 1)
                dve.scalar_tensor_tensor(out=wa_l[:, part], in0=stage_att[:, part], scalar=WS, in1=wa_h[:, part],
                                         op0=ALU.mult, op1=ALU.subtract).then_inc(S[f"{n}_lo"], 1)
                if n == "att_k":
                    split_lo(0, 0)
            dve.wait_ge(S["bias_in"], 32)
            dve.tensor_scalar(bias1[:], bias[:, 0:2, :], 1.0, None, ALU.add).then_inc(S["bias_done"], 1)
            dve.tensor_scalar(bias_v[:], bias[:, 2, :], WS, None, ALU.mult).then_inc(S["bias_done"], 1)
            dve.wait_ge(S["bias_done"], 2)
            dve.wait_ge(S["x1_in"], 16)
            dve.wait_ge(S["const_dve"], 6)
            step(0, False, True)
            dve.wait_ge(S["x_in"], 16)
            step(1, True, True)
            with dve.Fori(2, B - 1) as i:
                step(i, True, True, True)
            step(B - 1, True, False, True)
            for k in range(4):
                logits(B - 1, k)
            dve.wait_ge(S["best_done"], 2 * B)

            n = [0]

            def then(ins, wait=True):
                n[0] += 1
                ins.then_inc(S["rt"], 1)
                if wait:
                    dve.wait_ge(S["rt"], n[0])

            over = lambda a, m: a.rearrange("p (o m) -> p o m", o=1).to_broadcast((P, m, a.shape[1]))
            wide = lambda a, m: a.rearrange("p (m o) -> p m o", o=1).to_broadcast((P, a.shape[1], m))
            flat = lambda a: a.rearrange("p a b -> p (a b)")
            dve.tensor_tensor(sc_d[:], best[:, 1, :], best[:, 0, :], ALU.subtract).then_inc(S["dscore"], 1)
            then(dve.tensor_tensor(oh[:].rearrange("p k t e -> p (k t) e"), over(iota_f[:, 0:E], 2 * NT),
                                   wide(flat(ei[:]), E), ALU.is_equal))
            by_tile = lambda a: a.rearrange("p e t -> p t e")
            dve.tensor_tensor(by_tile(member[:]), oh[:, 0, :, :], oh[:, 1, :, :], ALU.add).then_inc(S["member_done"], 1)
            expert_lo(E - 2, 2)
            for k in range(2):
                then(dve.tensor_copy(vals[:, 0, k * NT:(k + 1) * NT], tok_f[:]), wait=False)
            dve.wait_ge(S["rank_ps"], 1)
            then(dve.tensor_reduce(count[:], total, AX.X, ALU.add), wait=False)
            then(dve.tensor_tensor_scan(flat(run), ones16[:], flat(total), 0.0, ALU.mult, ALU.add))
            then(dve.tensor_tensor(cmp, wide(count[:], NT), over(full_f[:], E), ALU.is_gt), wait=False)
            dve.wait_ge(S["escore"], 1)
            then(dve.tensor_scalar(sc_1[:], sc_e[:], 1.0, None, ALU.add))
            then(dve.tensor_reduce(nblk[:], cmp, AX.X, ALU.add), wait=False)
            then(dve.reciprocal(score[:, 0, :], sc_1[:]))
            then(dve.tensor_tensor_scan(bend[:], ones16[:, 0:E], nblk[:], 0.0, ALU.mult, ALU.add), wait=False)
            then(dve.tensor_tensor(s1, run, total, ALU.subtract))
            then(dve.tensor_tensor(r1[:], bend[:], nblk[:], ALU.subtract), wait=False)
            then(dve.tensor_tensor(r2[:], run[:, :, NT - 1], count[:], ALU.subtract), wait=False)
            then(dve.tensor_tensor(s2, s1, before, ALU.add))
            then(dve.scalar_tensor_tensor(out=base[:], in0=r1[:], scalar=float(P), in1=r2[:], op0=ALU.mult, op1=ALU.subtract),
                 wait=False)
            then(dve.tensor_tensor(score[:, 1, :], sc_e[:], score[:, 0, :], ALU.mult))
            then(dve.tensor_tensor(s3, s2, wide(base[:], NT), ALU.add), wait=False)
            then(dve.tensor_copy(vals[:, 1, :], flat(score[:])))
            for k in range(2):
                then(dve.tensor_tensor(pick[:, k, :, :], oh[:, k, :, :], by_tile(s3), ALU.mult), wait=False)
            then(dve.tensor_tensor(vals[:, 2, :], flat(score[:]), vals[:, 1, :], ALU.subtract))
            then(dve.tensor_reduce(slot[:], pick[:].rearrange("p k t e -> p (k t) e"), AX.X, ALU.add), wait=False)
            shared_out(B - 2)
            dve.wait_ge(S["rt"], n[0])
            then(dve.tensor_copy(slot_i[:], slot[:]))
            then(dve.tensor_scalar(pos_i[:], slot_i[:], P - 1, None, ALU.bitwise_and), wait=False)
            then(dve.tensor_scalar(blk_i[:], slot_i[:], 7, None, ALU.arith_shift_right))
            dve.tensor_copy(pos_f[:], pos_i[:]).then_inc(S["pos_done"], 1)
            then(dve.tensor_copy(blk16[:], blk_i[:]))
            dve.wait_ge(S["iota_blk_done"], 1)
            then(dve.tensor_tensor(at_blk, iota_blk[:], over(blk16[:], NBP), ALU.is_equal))
            for j in range(3):
                then(dve.tensor_tensor(put[:, j * NBP:(j + 1) * NBP, :], at_blk, over(vals[:, j, :], NBP), ALU.mult), wait=False)
            dve.wait_ge(S["pos_done"], 1)
            for m in range(POOL_TILES, 2 * NT):
                ins = dve.tensor_scalar(at_pos[m], iota16[:], pos_f[:, m:m + 1], None, ALU.is_equal)
            ins.then_inc(S["put_done"], 1)
            expert_lo(E - 1, 0)
            then(dve.tensor_tensor(bcmp[:], wide(iota_f[:, 0:NBP], E), over(bend[:], NBP), ALU.is_ge))
            then(dve.tensor_reduce(bexp[:], bcmp[:], AX.X, ALU.add), wait=False)
            dve.wait_ge(S["put_ps"], 1)
            then(dve.tensor_scalar(src_f[:], bV[:, 0:NBP], -1.0, 0.0, ALU.add, ALU.max))
            dve.tensor_copy(src_row[:], src_f[:]).then_inc(S["plan_done"], 1)
            then(dve.tensor_scalar(bexp_c[:], bexp[:], float(E - 1), None, ALU.min), wait=False)
            act_lo(B - 1, NP - 1)
            then(dve.tensor_scalar(pad_f[:], bV[:, 0:NBP], 0.0, float(BIG), ALU.is_equal, ALU.mult), wait=False)
            then(dve.tensor_scalar(slot_lo[:], bV[:, 2 * NBP:3 * NBP], 1.0 / WS, None, ALU.mult))
            dve.tensor_copy(blk_expert[:], bexp_c[:]).then_inc(S["bexp_done"], 1)
            then(dve.scalar_tensor_tensor(out=dst_f[:], in0=bV[:, 0:NBP], scalar=-1.0, in1=pad_f[:], op0=ALU.add, op1=ALU.add))
            dve.tensor_copy(dst_row[:], dst_f[:]).then_inc(S["plan_done"], 1)
            dve.scalar_tensor_tensor(out=slot_score[:], in0=bV[:, NBP:2 * NBP], scalar=1.0 / WS, in1=slot_lo[:],
                                     op0=ALU.mult, op1=ALU.add).then_inc(S["plan_done"], 1)
            dve.wait_ge(S["plan_done"], 3)
            for j in range(1, 3):
                expert_lo(E - 1, j)

            def gather_lo(b, q):
                dve.wait_ge(S["gh_done"], b + 1)
                dve.tensor_tensor(gT_l[q].rearrange("p k l -> p (k l)"), bT[:, 0:KC * P],
                                  gT_h[q].rearrange("p k l -> p (k l)"), ALU.subtract).then_inc(S["gl_done"], 1)

            def routed_act_lo(b, q):
                dve.wait_ge(S["ah_done"], NP * B + b + 1)
                dve.tensor_tensor(al[q][:], bK[:], ah[q][:], ALU.subtract).then_inc(S["al_done"], 1)

            def result(b, q):
                dve.wait_ge(S["yl_done"], b + 1)
                if not isinstance(b, int) or b >= 2:
                    dve.wait_ge(S["scattered"], 16 * (b - 1))
                dve.scalar_tensor_tensor(out=ya[q], in0=(bV, bQ)[q][:, 0:D], scalar=slot_score[:, bass.ds(b, 1)],
                                         in1=yl[q], op0=ALU.mult, op1=ALU.add).then_inc(S["y_done"], 1)

            def routed(b, q, first, last):
                if not first:
                    routed_act_lo(b - 1, 1 - q)
                if not last:
                    gather_lo(b + 1, 1 - q)
                swiglu(NP * B + b, q)
                if not first:
                    result(b - 1, 1 - q)

            gather_lo(0, 0)
            shared_out(B - 1)
            routed(0, 0, True, False)
            routed(1, 1, False, False)
            routed(2, 0, False, False)
            with dve.Fori(3, NBLK - 2, 2) as b:
                routed(b, 1, False, False)
                routed(b + 1, 0, False, False)
            routed(NBLK - 2, 1, False, False)
            routed(NBLK - 1, 0, False, True)
            routed_act_lo(NBLK - 1, 0)
            result(NBLK - 1, 0)


def kernel(**inputs):
    import numpy as np
    import concourse.bacc as bacc
    from concourse.bass_utils import run_bass_kernel_spmd

    a = {k: np.asarray(v) for k, v in inputs.items()}

    def rows(w):
        return w.reshape(-1, P, w.shape[-1]).transpose(1, 0, 2).reshape(P, -1)

    att = [rows(a[f"L0_attn_W{m}"].T) for m in "kqvo"] + [rows(a["L0_ffn_router_w"])]
    w1, w2 = a["L0_ffn_w1"], a["L0_ffn_w2"]
    arrays = {
        "x": a["L0_attn_x"],
        "w_att": np.concatenate(att, axis=1),
        "w_bias": np.stack([a[f"L0_attn_b{m}"].reshape(-1, P).T for m in "qkv"], axis=1),
        "w_bo": a["L0_attn_bo"].reshape(1, -1),
        "w_shared": np.stack([rows(a[f"L0_ffn_w_{m}"]) for m in ("gate", "up", "down")], axis=1),
        "w_expert": np.stack([np.concatenate([rows(w1[e]), rows(w2[e])], axis=1) for e in range(w1.shape[0])]),
    }
    arrays = {f"in_{k}": np.ascontiguousarray(v) for k, v in arrays.items()}
    nc = bacc.Bacc("TRN2", target_bir_lowering=False, num_devices=1)
    args = [nc.dram_tensor(k, v.shape, mybir.dt.from_np(v.dtype), kind="ExternalInput").ap() for k, v in arrays.items()]
    out = nc.dram_tensor("out_y", a["L0_attn_x"].shape, F32, kind="ExternalOutput").ap()
    layer_kernel(nc, *args, out)
    r = run_bass_kernel_spmd(nc, [arrays], core_ids=[0])
    return r.results[0]["out_y"]
```
